# Optimizing a Trainium2 kernel written in Bass

```python
import numpy as np
import jax
import jax.numpy as jnp

def _softmax(x, axis=-1):
    return jax.nn.softmax(x, axis=axis)

def _gelu(x):
    return jax.nn.gelu(x, approximate=True)

def _silu(x):
    return jax.nn.silu(x)

def _sigmoid(x):
    return jax.nn.sigmoid(x)

def _layernorm(x, axis=-1, eps=1e-05):
    m = jnp.mean(x, axis=axis, keepdims=True)
    v = jnp.var(x, axis=axis, keepdims=True)
    return (x - m) / jnp.sqrt(v + eps)

def _scatter_add(tgt, idx, src, axis=0):
    return tgt.at[idx].add(src)

def _segment_sum(src, seg, n):
    return jax.ops.segment_sum(src, seg, n)
kernel_name = 'mk_macaron_d1_jaxref_r8_aba1bb'

def setup_inputs(seed: int=0):
    np.random.seed(seed)
    _w = jnp.asarray

    def _L0_attn_setup():
        import jax, jax.numpy as jnp
        import numpy as np
        D_K, D_MODEL, NUM_HEADS = (64, 128, 16)

        def _xavier(key, shape):
            fan_in, fan_out = (shape[-2], shape[-1])
            limit = float(np.sqrt(6.0 / (fan_in + fan_out)))
            return jax.random.uniform(key, shape, jnp.float32, -limit, limit)
        key = jax.random.key(seed)
        kx, kq, kk, kv, ko = jax.random.split(key, 5)
        x = jax.random.normal(kx, (2, 256, D_MODEL), dtype=jnp.float32)
        w_q = _xavier(kq, (NUM_HEADS, D_MODEL, D_K))
        w_k = _xavier(kk, (NUM_HEADS, D_MODEL, D_K))
        w_v = _xavier(kv, (NUM_HEADS, D_MODEL, D_K))
        w_o = _xavier(ko, (NUM_HEADS * D_K, D_MODEL))
        return {'x': x, 'w_q': w_q, 'w_k': w_k, 'w_v': w_v, 'w_o': w_o}
    _L0_attn_in = _L0_attn_setup()

    def _L0_ffn_setup():
        import jax, jax.numpy as jnp
        import numpy as np
        B, L, H, E, I = (4, 256, 128, 8, 512)
        S = B * L
        CAP_FACTOR_EVAL = 2.0
        MIN_CAP = 4
        _cap = int(np.floor(CAP_FACTOR_EVAL * S / E))
        _cap += _cap % 2
        CAPACITY = max(_cap, MIN_CAP)

        def _layer_norm(x, g, b, eps=1e-05):
            mu = x.mean(-1, keepdims=True)
            var = ((x - mu) ** 2).mean(-1, keepdims=True)
            return (x - mu) * jax.lax.rsqrt(var + eps) * g + b
        key = jax.random.key(seed)
        ks = jax.random.split(key, 8)
        gate_std = float(np.sqrt(0.1 / H))
        return {'inputs': jax.random.normal(ks[0], (B, L, H), jnp.float32), 'gate_weight': jax.random.normal(ks[1], (E, H), jnp.float32) * gate_std, 'ln_gamma': jnp.ones((H,), jnp.float32), 'ln_beta': jnp.zeros((H,), jnp.float32), 'wi': jax.random.normal(ks[2], (E, H, I), jnp.float32) * float(1.0 / np.sqrt(H)), 'wo': jax.random.normal(ks[3], (E, I, H), jnp.float32) * float(1.0 / np.sqrt(I)), 'conf_w1': jax.random.normal(ks[4], (H // 2, H), jnp.float32) * float(np.sqrt(2.0 / (H + H // 2))), 'conf_b1': -jnp.ones((H // 2,), jnp.float32), 'conf_w2': jax.random.normal(ks[5], (1, H // 2), jnp.float32) * float(np.sqrt(2.0 / (1 + H // 2))), 'conf_b2': -jnp.ones((1,), jnp.float32), 'comp_w': jax.random.normal(ks[6], (1, H), jnp.float32) * float(1.0 / np.sqrt(H)), 'comp_b': jnp.zeros((1,), jnp.float32)}
    _L0_ffn_in = _L0_ffn_setup()
    _d = {'L0_attn_x': _L0_attn_in['x'], 'L0_attn_w_q': _L0_attn_in['w_q'], 'L0_attn_w_k': _L0_attn_in['w_k'], 'L0_attn_w_v': _L0_attn_in['w_v'], 'L0_attn_w_o': _L0_attn_in['w_o'], 'L0_ffn_gate_weight': _L0_ffn_in['gate_weight'], 'L0_ffn_ln_gamma': _L0_ffn_in['ln_gamma'], 'L0_ffn_ln_beta': _L0_ffn_in['ln_beta'], 'L0_ffn_wi': _L0_ffn_in['wi'], 'L0_ffn_wo': _L0_ffn_in['wo'], 'L0_ffn_conf_w1': _L0_ffn_in['conf_w1'], 'L0_ffn_conf_b1': _L0_ffn_in['conf_b1'], 'L0_ffn_conf_w2': _L0_ffn_in['conf_w2'], 'L0_ffn_conf_b2': _L0_ffn_in['conf_b2'], 'L0_ffn_comp_w': _L0_ffn_in['comp_w'], 'L0_ffn_comp_b': _L0_ffn_in['comp_b']}
    _x0 = _d['L0_attn_x']
    _d['L0_attn_x'] = jax.random.normal(jax.random.fold_in(jax.random.key(seed), 1), (16, 256, 128), dtype=_x0.dtype)
    del _x0
    return _d

def reference(L0_attn_x, L0_attn_w_q, L0_attn_w_k, L0_attn_w_v, L0_attn_w_o, L0_ffn_gate_weight, L0_ffn_ln_gamma, L0_ffn_ln_beta, L0_ffn_wi, L0_ffn_wo, L0_ffn_conf_w1, L0_ffn_conf_b1, L0_ffn_conf_w2, L0_ffn_conf_b2, L0_ffn_comp_w, L0_ffn_comp_b):

    def _L0_attn_ref(x, w_q, w_k, w_v, w_o):
        import jax, jax.numpy as jnp
        import numpy as np
        D_K, D_MODEL, NUM_HEADS = (64, 128, 16)

        def _xavier(key, shape):
            fan_in, fan_out = (shape[-2], shape[-1])
            limit = float(np.sqrt(6.0 / (fan_in + fan_out)))
            return jax.random.uniform(key, shape, jnp.float32, -limit, limit)
        scale = 1.0 / jnp.sqrt(jnp.asarray(D_K, dtype=jnp.float32))
        q = jnp.einsum('bsd,hdk->bhsk', x, w_q)
        k = jnp.einsum('bsd,hdk->bhsk', x, w_k)
        v = jnp.einsum('bsd,hdk->bhsk', x, w_v)
        scores = jnp.einsum('bhqk,bhmk->bhqm', q, k) * scale
        weights = jax.nn.softmax(scores, axis=-1)
        z = jnp.einsum('bhqm,bhmk->bhqk', weights, v)
        b, h, s, dk = z.shape
        z = jnp.transpose(z, (0, 2, 1, 3)).reshape(b, s, h * dk)
        z = jnp.einsum('bse,ed->bsd', z, w_o)
        return x + z

    def _L0_ffn_ref(inputs, gate_weight, ln_gamma, ln_beta, wi, wo, conf_w1, conf_b1, conf_w2, conf_b2, comp_w, comp_b):
        import jax, jax.numpy as jnp
        import numpy as np
        B, L, H, E, I = (4, 256, 128, 8, 512)
        S = B * L
        CAP_FACTOR_EVAL = 2.0
        MIN_CAP = 4
        _cap = int(np.floor(CAP_FACTOR_EVAL * S / E))
        _cap += _cap % 2
        CAPACITY = max(_cap, MIN_CAP)

        def _layer_norm(x, g, b, eps=1e-05):
            mu = x.mean(-1, keepdims=True)
            var = ((x - mu) ** 2).mean(-1, keepdims=True)
            return (x - mu) * jax.lax.rsqrt(var + eps) * g + b
        tokens = inputs.reshape(-1, H)
        residual = tokens
        tokens = _layer_norm(tokens, ln_gamma, ln_beta)
        complexity_score = jax.nn.sigmoid(tokens @ comp_w.T + comp_b).mean()
        hdn = jax.nn.relu(tokens @ conf_w1.T + conf_b1)
        confidence_score = jax.nn.sigmoid(hdn @ conf_w2.T + conf_b2).mean()
        logits = tokens.astype(jnp.float32) @ gate_weight.astype(jnp.float32).T
        probs = jax.nn.softmax(logits, axis=-1)
        top1 = jnp.argmax(logits, axis=-1)
        onehot = jax.nn.one_hot(top1, E, dtype=jnp.int32)
        rank_e = jnp.cumsum(onehot, axis=0) - onehot
        rank = jnp.sum(rank_e * onehot, axis=-1)
        keep = rank < CAPACITY
        weight = jnp.take_along_axis(probs, top1[:, None], axis=-1)[:, 0]
        weight = (weight * keep).astype(tokens.dtype)
        slot = jnp.where(keep, rank, 0)
        dispatch = jnp.zeros((E, CAPACITY, H), tokens.dtype)
        dispatch = dispatch.at[top1, slot].add(tokens * keep[:, None])
        h = jax.nn.gelu(jnp.einsum('ech,ehi->eci', dispatch, wi), approximate=False)
        expert_out = jnp.einsum('eci,eih->ech', h, wo)
        combined = weight[:, None] * expert_out[top1, slot]
        out = (residual + combined).reshape(inputs.shape)
        return out
    x = L0_attn_x
    x = x + 0.5 * _L0_ffn_ref(_layernorm(x, axis=-1), L0_ffn_gate_weight, L0_ffn_ln_gamma, L0_ffn_ln_beta, L0_ffn_wi, L0_ffn_wo, L0_ffn_conf_w1, L0_ffn_conf_b1, L0_ffn_conf_w2, L0_ffn_conf_b2, L0_ffn_comp_w, L0_ffn_comp_b)
    x = x + _L0_attn_ref(_layernorm(x, axis=-1), L0_attn_w_q, L0_attn_w_k, L0_attn_w_v, L0_attn_w_o)
    x = x + 0.5 * _L0_ffn_ref(_layernorm(x, axis=-1), L0_ffn_gate_weight, L0_ffn_ln_gamma, L0_ffn_ln_beta, L0_ffn_wi, L0_ffn_wo, L0_ffn_conf_w1, L0_ffn_conf_b1, L0_ffn_conf_w2, L0_ffn_conf_b2, L0_ffn_comp_w, L0_ffn_comp_b)
    return x

_drawn_inputs = setup_inputs


def setup_inputs(seed=0):
    import zlib

    import numpy as np

    out = dict(_drawn_inputs(seed))
    spreads = {'L0_ffn_ln_gamma': (1.0, 0.6),
     'L0_ffn_ln_beta': (0.0, 0.395),
     'L0_ffn_conf_b1': (-1.0, 0.2)}
    factors = {}
    for name, (base, spread) in spreads.items():
        noise = np.random.default_rng([zlib.crc32(name.encode()), seed]).standard_normal(out[name].shape)
        drawn = base * np.exp(spread * noise) if base else spread * noise
        out[name] = jnp.asarray(drawn.astype(out[name].dtype))
    for name, factor in factors.items():
        out[name] = (out[name] * factor).astype(out[name].dtype)
    return out
```

```python
import numpy as np
import concourse.bass as bass
from concourse import mybir
from contextlib import ExitStack

F32 = mybir.dt.float32
F32R = mybir.dt.float32r
BF16 = mybir.dt.bfloat16
I32 = mybir.dt.int32
ALU = mybir.AluOpType
ACT = mybir.ActivationFunctionType
AX = mybir.AxisListType

P = 128
D = 128
NB, SEQ = 16, 256
NT = NB * SEQ // P
NH, DK = 16, 64
NPAIR = NH // 2
NE, FF = 8, 512
CAP = 256
SLOTS = NE * CAP
NI = FF // P
GT = 8
NG = NT // GT
BT = SEQ // P
EPS = 1e-5
SCALE = 1.0 / float(np.sqrt(DK))
NOSLOT = 2 * SLOTS


def macaron_kernel(nc, x, w_qT, w_kT, w_v, w_o, gate, gamma, beta, wi, wo, ident_in, before_in, ebase_in, rev_in,
                   noslot_in, out):
    ctx = ExitStack()
    with ctx:
        def sb(name, shape, dt=F32):
            return ctx.enter_context(nc.sbuf_tensor(name, shape, dt))

        def sem(name):
            return ctx.enter_context(nc.semaphore(name))

        X = sb("X", [P, NT, D])
        ident = sb("ident", [P, P])
        before = sb("before", [P, P], BF16)
        ones = sb("ones", [P, P], BF16)
        tri_f = sb("tri_f", [P, P])
        ebase = sb("ebase", [P, NE])
        rev = sb("rev", [P, NE])
        noslot = sb("noslot", [P, GT])
        gcol = sb("gcol", [P, 1])
        bcol = sb("bcol", [P, 1])
        gateT = sb("gateT", [P, NE])
        mhalf = sb("mhalf", [P, GT])
        epsc = sb("epsc", [P, GT])
        wqT = sb("wqT", [P, NPAIR, D])
        wkT = sb("wkT", [P, NPAIR, D])
        wv = sb("wv", [P, NH * DK])
        wvh = sb("wvh", [P, NH * DK], F32R)
        wvl = sb("wvl", [P, NH * DK], F32R)
        wos = sb("wos", [P, NPAIR, D])
        ah = sb("ah", [P, NH, D], F32R)
        al = sb("al", [P, NH, D], F32R)
        class Routing:
            pass
        rt = []
        for f, n in ((0, GT), (1, BT)):
            r = Routing()
            r.n = n
            r.st = sb(f"r{f}_st", [P, n, 6])
            r.mean = sb(f"r{f}_mean", [P, n])
            r.diff = sb(f"r{f}_diff", [P, n])
            r.m2 = sb(f"r{f}_m2", [P, n])
            r.var = sb(f"r{f}_var", [P, n])
            r.vare = sb(f"r{f}_vare", [P, n])
            r.rs = sb(f"r{f}_rs", [P, n])
            r.t1 = sb(f"r{f}_t1", [P, n])
            r.t2 = sb(f"r{f}_t2", [P, n])
            r.t3 = sb(f"r{f}_t3", [P, n])
            r.rs2 = sb(f"r{f}_rs2", [P, n])
            r.rst = sb(f"r{f}_rst", [P, n])
            r.y = sb(f"r{f}_y", [P, n, D])
            r.tok = sb(f"r{f}_tok", [P, n, D])
            r.tokT = sb(f"r{f}_tokT", [P, n, P])
            r.lmax = sb(f"r{f}_lmax", [P, n])
            r.dlt = sb(f"r{f}_dlt", [P, n, NE])
            r.exl = sb(f"r{f}_exl", [P, n, NE])
            r.cand = sb(f"r{f}_cand", [P, n, NE])
            r.cmax = sb(f"r{f}_cmax", [P, n])
            r.hot = sb(f"r{f}_hot", [P, n, NE], BF16)
            r.hotf = sb(f"r{f}_hotf", [P, n, NE])
            r.seen = sb(f"r{f}_seen", [P, NE])
            r.rk = sb(f"r{f}_rk", [P, n, NE])
            r.rsel = sb(f"r{f}_rsel", [P, n, NE])
            r.bsel = sb(f"r{f}_bsel", [P, n, NE])
            r.rank = sb(f"r{f}_rank", [P, n])
            r.base = sb(f"r{f}_base", [P, n])
            r.keep = sb(f"r{f}_keep", [P, n])
            r.den = sb(f"r{f}_den", [P, n])
            r.rden = sb(f"r{f}_rden", [P, n])
            r.d1 = sb(f"r{f}_d1", [P, n])
            r.d2 = sb(f"r{f}_d2", [P, n])
            r.d3 = sb(f"r{f}_d3", [P, n])
            r.dest = sb(f"r{f}_dest", [P, n], I32)
            r.src = sb(f"r{f}_src", [P, NT], I32)
            r.wt = sb(f"r{f}_wt", [P, NT])
            rt.append(r)
        ein = [sb(f"ein{i}", [P, 2, D]) for i in range(2)]
        ewi = [sb(f"ewi{i}", [P, FF]) for i in range(2)]
        ewo = [sb(f"ewo{i}", [P, NI, D]) for i in range(2)]
        einT = [sb(f"einT{i}", [P, CAP]) for i in range(2)]
        ehT = [sb(f"ehT{i}", [P, NI, CAP]) for i in range(2)]
        eres = [sb(f"eres{i}", [P, 2, D]) for i in range(2)]
        gidx = [sb(f"gidx{i}", [P, BT], I32) for i in range(2)]
        got = [sb(f"got{i}", [P, BT, D]) for i in range(2)]
        res = [sb(f"res{i}", [P, BT, D]) for i in range(2)]
        zrow = sb("zrow", [P, SLOTS * D // P // 4])
        c_st = sb("c_st", [P, BT, 6])
        c_mean, c_diff, c_m2, c_varr, c_vare, c_rs = [sb(f"c_{k}", [P, BT]) for k in
                                                      ("mean", "diff", "m2", "varr", "vare", "rs")]
        ya = sb("ya", [P, BT, D])
        x1 = sb("x1", [P, BT, D])
        x2 = sb("x2", [P, BT, D])
        yTh = [sb(f"yTh{i}", [P, SEQ], F32R) for i in range(2)]
        yTl = [sb(f"yTl{i}", [P, SEQ], F32R) for i in range(2)]
        Gh = [sb(f"Gh{i}", [P, 2 * SEQ], F32R) for i in range(2)]
        Gl = [sb(f"Gl{i}", [P, 2 * SEQ], F32R) for i in range(2)]
        V = sb("V", [P, BT, NH * DK])
        mx = [sb(f"mx{i}", [P, 4]) for i in range(4)]
        nbias = [sb(f"nbias{i}", [P, 4]) for i in range(4)]
        sums = [sb(f"sums{i}", [P, 4]) for i in range(4)]
        rsum = [sb(f"rsum{i}", [P, 4]) for i in range(4)]
        prob = [sb(f"prob{i}", [P, 2, 2, SEQ]) for i in range(4)]
        probT = [[sb(f"probT{i}{h}", [P, 2, SEQ]) for h in range(2)] for i in range(2)]
        zT = [sb(f"zT{i}", [P, NPAIR, SEQ]) for i in range(2)]
        SC = [[ctx.enter_context(nc.psum_tensor(f"SC{i}{c}", [P, 512], F32)) for c in range(2)] for i in range(2)]
        PT = [ctx.enter_context(nc.psum_tensor(f"PT{h}", [P, 512], F32)) for h in range(2)]
        PJ = ctx.enter_context(nc.psum_tensor("PJ", [P, 512], F32))
        Z = ctx.enter_context(nc.psum_tensor("Z", [P, 512], F32))
        disp = nc.dram_tensor("disp", [SLOTS, D], F32, kind="Internal").ap()
        eout = nc.dram_tensor("eout", [SLOTS, D], F32, kind="Internal").ap()

        x_in = [sem(f"x_in{g}") for g in range(NG)]
        const_in, watt_in, consts = sem("const_in"), sem("watt_in"), sem("consts")
        before_ready = sem("before_ready")
        zrow_set, disp_zeroed = sem("zrow_set"), sem("disp_zeroed")
        a_ps, a_hi, a_lo, wv_hi, wv_lo = sem("a_ps"), sem("a_hi"), sem("a_lo"), sem("wv_hi"), sem("wv_lo")
        R = []
        for f in range(2):
            R.append({k: sem(f"f{f}_{k}") for k in (
                "stats", "var_ready", "rstd_ready", "norm", "y_done", "tok_done", "tT_ps", "tT_ready", "logit_ps",
                "delta_ready", "exl_ready", "hot_ready", "hots", "rank_ps", "seen_done", "final", "dest_ready",
                "pool", "scattered", "first", "x_done")})
        ein_in, ein_ps, ein_ready = [sem(f"ein_in{i}") for i in range(2)], sem("ein_ps"), sem("ein_ready")
        up_ps, gelu_done, down_ps, eres_ready = sem("up_ps"), sem("gelu_done"), sem("down_ps"), sem("eres_ready")
        eres_out = [sem(f"eres_out{i}") for i in range(2)]
        idx_ready, combined = sem("idx_ready"), sem("combined")
        got_in = [sem(f"got_in{i}") for i in range(2)]
        c_stats, c_var, c_rstd, c_chain = sem("c_stats"), sem("c_var"), sem("c_rstd"), sem("c_chain")
        ya_ready, x_plus_ya = sem("ya_ready"), sem("x_plus_ya")
        yT_ps, yT_hi, yT_lo = sem("yT_ps"), sem("yT_hi"), sem("yT_lo")
        g_ps, g_hi, g_lo = sem("g_ps"), sem("g_hi"), sem("g_lo")
        v_ps, v_ready = sem("v_ps"), sem("v_ready")
        scores_ps, max_done, bias_ready = sem("scores_ps"), sem("max_done"), sem("bias_ready")
        exp_done, rsum_ready, prob_ready = sem("exp_done"), sem("rsum_ready"), sem("prob_ready")
        pT_ps, pT_even, pT_odd = sem("pT_ps"), sem("pT_even"), sem("pT_odd")
        z_ps, z_ready = sem("z_ps"), sem("z_ready")
        o_ps, o_added = sem("o_ps"), sem("o_added")
        gi2, comb2 = sem("gi2"), sem("comb2")
        got2, out_sent = [sem(f"got2_{i}") for i in range(2)], [sem(f"out_sent{i}") for i in range(2)]

        block = ctx.enter_context(nc.Block())

        ABANK = [SC[1][0], SC[1][1], PT[0], PT[1]]

        def heads4(t, q):
            return t[:, 8 * (q // 2):8 * (q // 2) + 8, :].rearrange("p (k two) d -> p k two d", two=2)[:, :, q % 2, :]

        def four(bank):
            return bank[:].rearrange("p (k d) -> p k d", k=4)

        def bc(ap, n):
            return ap.unsqueeze(2).to_broadcast([P, ap.shape[1], n])


        N_STATS = 6

        def dve_var(dve, stats, chain_sem, mean, diff, m2, vare, var, base, done):
            k = base
            nc.vector.tensor_tensor(mean, stats[:, :, 1], stats[:, :, 4], ALU.add).then_inc(chain_sem, 1)
            nc.vector.tensor_tensor(diff, stats[:, :, 1], stats[:, :, 4], ALU.subtract).then_inc(chain_sem, 1)
            nc.vector.tensor_tensor(m2, stats[:, :, 2], stats[:, :, 5], ALU.add).then_inc(chain_sem, 1)
            dve.wait_ge(chain_sem, k + 2)
            nc.vector.scalar_tensor_tensor(diff, diff, 0.25, diff, ALU.mult, ALU.mult).then_inc(chain_sem, 1)
            nc.vector.tensor_scalar(mean, mean, 0.5, None, ALU.mult).then_inc(chain_sem, 1)
            dve.wait_ge(chain_sem, k + 4)
            nc.vector.scalar_tensor_tensor(var, m2, 1.0 / D, diff, ALU.mult, ALU.add).then_inc(chain_sem, 1)
            dve.wait_ge(chain_sem, k + 6)
            nc.vector.tensor_scalar(vare, var, EPS, None, ALU.add).then_inc(done, 1)

        def route_stats(dve, f, i, xs):
            r, s = rt[f], R[f]
            for j in range(r.n):
                ins = nc.vector.bn_stats(r.st[:, j, :], xs[:, j, :])
            ins.then_inc(s["first"], 1)
            dve.wait_ge(s["first"], i + 1)
            dve_var(dve, r.st, s["stats"], r.mean[:], r.diff[:], r.m2[:], r.vare[:], r.var[:],
                    i * N_STATS, s["var_ready"])

        def route_rstd(pool, f, i):
            r, s, b = rt[f], R[f], i * 4
            pool.wait_ge(s["var_ready"], i + 1)
            nc.gpsimd.tensor_tensor(r.rs[:], r.vare[:], mhalf[:, 0:r.n], ALU.pow).then_inc(s["pool"], 1)
            pool.wait_ge(s["pool"], b + 1)
            nc.gpsimd.tensor_tensor(r.t1[:], r.rs[:], r.rs[:], ALU.mult).then_inc(s["pool"], 1)
            pool.wait_ge(s["pool"], b + 2)
            nc.gpsimd.tensor_tensor(r.t2[:], r.t1[:], r.var[:], ALU.mult).then_inc(s["pool"], 1)
            pool.wait_ge(s["pool"], b + 3)
            nc.gpsimd.tensor_tensor(r.t3[:], r.t2[:], epsc[:, 0:r.n], ALU.add).then_inc(s["pool"], 1)
            pool.wait_ge(s["pool"], b + 4)
            nc.gpsimd.tensor_tensor(r.rs2[:], r.t3[:], mhalf[:, 0:r.n], ALU.pow).then_inc(s["rstd_ready"], 1)

        def route_norm(dve, f, i, xs, xo):
            r, s = rt[f], R[f]
            dve.wait_ge(s["rstd_ready"], i + 1)
            nc.vector.tensor_tensor(r.rst[:], r.rs[:], r.rs2[:], ALU.mult).then_inc(s["norm"], 1)
            for j in range(r.n):
                ins = nc.vector.tensor_scalar(r.y[:, j, :], xs[:, j, :], r.mean[:, j:j + 1], r.rs[:, j:j + 1],
                                              ALU.subtract, ALU.mult)
            ins.then_inc(s["y_done"], 1)
            dve.wait_ge(s["norm"], i + 1)
            if not (isinstance(i, int) and i == 0):
                dve.wait_ge(s["scattered"], i * r.n * 16)
            for j in range(r.n):
                ins = nc.vector.tensor_scalar(r.tok[:, j, :], xs[:, j, :], r.mean[:, j:j + 1], r.rst[:, j:j + 1],
                                              ALU.subtract, ALU.mult)
            ins.then_inc(s["tok_done"], 1)
            dve.wait_ge(s["y_done"], i + 1)
            dve.wait_ge(s["tok_done"], i + 1)
            nc.vector.scalar_tensor_tensor(xo, r.y[:, :, :], 0.5, xs[:, :, :], ALU.mult, ALU.add).then_inc(s["x_done"], 1)

        def route_pick(dve, f, i, logits):
            r, s = rt[f], R[f]
            b = i * 4
            dve.wait_ge(s["logit_ps"], i + 1)
            nc.vector.tensor_reduce(r.lmax[:], logits, AX.X, ALU.max).then_inc(s["hots"], 1)
            dve.wait_ge(s["hots"], b + 1)
            nc.vector.tensor_tensor(r.dlt[:], logits, bc(r.lmax[:], NE), ALU.subtract).then_inc(s["delta_ready"], 1)
            dve.wait_ge(s["delta_ready"], i + 1)
            nc.vector.scalar_tensor_tensor(r.cand[:], r.dlt[:], 0.0, rev[:].unsqueeze(1).to_broadcast([P, r.n, NE]),
                                           ALU.is_ge, ALU.mult).then_inc(s["hots"], 1)
            dve.wait_ge(s["hots"], b + 2)
            nc.vector.tensor_reduce(r.cmax[:], r.cand[:], AX.X, ALU.max).then_inc(s["hots"], 1)
            dve.wait_ge(s["hots"], b + 3)
            nc.vector.tensor_tensor(r.hotf[:], r.cand[:], bc(r.cmax[:], NE), ALU.is_equal).then_inc(s["hots"], 1)
            dve.wait_ge(s["hots"], b + 4)
            nc.vector.tensor_copy(r.hot[:], r.hotf[:]).then_inc(s["hot_ready"], 1)

        N_FINAL = 13

        def route_final(dve, f, i, ranks, tiles):
            r, s, n = rt[f], R[f], rt[f].n
            b = i * N_FINAL
            fin = s["final"]
            tt, ts, stt = nc.vector.tensor_tensor, nc.vector.tensor_scalar, nc.vector.scalar_tensor_tensor
            seen_b = r.seen[:].unsqueeze(1).to_broadcast([P, n, NE])
            dve.wait_ge(s["rank_ps"], i + 1)
            if not (isinstance(i, int) and i == 0):
                dve.wait_ge(s["seen_done"], i)
            else:
                dve.wait_ge(consts, 5)
            tt(r.rk[:], ranks[:, 0:n, :], seen_b, ALU.add).then_inc(fin, 1)
            tt(r.bsel[:], r.hotf[:], ebase[:].unsqueeze(1).to_broadcast([P, n, NE]), ALU.mult).then_inc(fin, 1)
            dve.wait_ge(s["exl_ready"], i + 1)
            nc.vector.tensor_reduce(r.den[:], r.exl[:], AX.X, ALU.add).then_inc(fin, 1)
            dve.wait_ge(fin, b + 1)
            tt(r.seen[:], ranks[:, n, :], r.seen[:], ALU.add).then_inc(s["seen_done"], 1)
            tt(r.rsel[:], r.rk[:], r.hotf[:], ALU.mult).then_inc(fin, 1)
            dve.wait_ge(fin, b + 3)
            nc.vector.tensor_reduce(r.base[:], r.bsel[:], AX.X, ALU.add).then_inc(fin, 1)
            nc.vector.reciprocal(r.rden[:], r.den[:]).then_inc(fin, 1)
            dve.wait_ge(fin, b + 4)
            nc.vector.tensor_reduce(r.rank[:], r.rsel[:], AX.X, ALU.add).then_inc(fin, 1)
            dve.wait_ge(fin, b + 7)
            ts(r.keep[:], r.rank[:], float(CAP), None, ALU.is_lt).then_inc(fin, 1)
            tt(r.d1[:], r.rank[:], r.base[:], ALU.add).then_inc(fin, 1)
            dve.wait_ge(fin, b + 9)
            tt(r.d2[:], r.d1[:], noslot[:, 0:n], ALU.subtract).then_inc(fin, 1)
            tt(r.d3[:], r.rank[:], r.keep[:], ALU.mult).then_inc(fin, 1)
            stt(r.wt[:, tiles], r.keep[:], 0.5, r.rden[:], ALU.mult, ALU.mult).then_inc(fin, 1)
            dve.wait_ge(fin, b + 10)
            tt(r.d2[:], r.d2[:], r.keep[:], ALU.mult).then_inc(fin, 1)
            dve.wait_ge(fin, b + 13)
            if not (isinstance(i, int) and i == 0):
                dve.wait_ge(s["scattered"], i * n * 16)
            tt(r.src[:, tiles], r.d3[:], r.base[:], ALU.add)
            tt(r.dest[:], r.d2[:], noslot[:, 0:n], ALU.add).then_inc(s["dest_ready"], 1)

        def route_scatter(pool, f):
            r, s = rt[f], R[f]
            for j in range(r.n):
                nc.gpsimd.indirect_dma_start(
                    out=disp[:, :], out_offset=bass.IndirectOffsetOnAxis(r.dest[:, j:j + 1], 0),
                    in_=r.tok[:, j, :], in_offset=None, bounds_check=SLOTS - 1,
                    oob_is_err=False).then_inc(s["scattered"], 16)

        def pe_ranks(f, ps):
            r = rt[f]
            for j in range(r.n + 1):
                srcs = list(range(min(j, r.n)))
                o = ps[:, j, :]
                first = True
                if j < r.n:
                    ins = nc.tensor.matmul(o, before[:], r.hot[:, j, :], start=True, stop=not srcs)
                    first = False
                for k in srcs:
                    ins = nc.tensor.matmul(o, ones[:], r.hot[:, k, :], start=first, stop=k == srcs[-1])
                    first = False
            return ins

        UPS = [[SC[1][0], SC[1][1]], [PT[0], PT[1]]]
        DNS = [PJ, Z]

        def sp_expert(sp, E, e, par, weights_only=False):
            if not (isinstance(E, int) and E < 2):
                sp.wait_ge(down_ps, E - 1)
            sp.dma_start(ewi[par][:], wi[e]).then_inc(ein_in[par], 16)
            sp.dma_start(ewo[par][:], wo[e].rearrange("(i p) d -> p i d", p=P)).then_inc(ein_in[par], 16)
            sp.dma_start(ein[par][:], disp[bass.ds(e * CAP, CAP), :].rearrange("(c p) d -> p c d", p=P)) \
                .then_inc(ein_in[par], 16)

        def pe_expert_in(pe, E, par):
            pe.wait_ge(ein_in[par], 24 * (E - par) + 48)
            if not (isinstance(E, int) and E < 2):
                pe.wait_ge(ein_ready, E - 1)
            for c in range(2):
                ins = nc.tensor.transpose(SC[0][par][:, c * P:(c + 1) * P], ein[par][:, c, :], ident[:])
            ins.then_inc(ein_ps, 1)

        def pe_expert_up(pe, E, par):
            pe.wait_ge(ein_ready, E + 1)
            if not (isinstance(E, int) and E < 2):
                pe.wait_ge(gelu_done, 2 * E - 2)
            for i in range(NI):
                ins = nc.tensor.matmul(UPS[par][i // 2][:, (i % 2) * CAP:(i % 2 + 1) * CAP],
                                       ewi[par][:, i * P:(i + 1) * P], einT[par][:], start=True, stop=True)
                if i % 2:
                    ins.then_inc(up_ps, 1)

        def pe_expert_down(pe, E, par):
            pe.wait_ge(gelu_done, 2 * E + 2)
            if not (isinstance(E, int) and E < 2):
                pe.wait_ge(eres_ready, E - 1)
            for c in range(2):
                for i in range(NI):
                    ins = nc.tensor.matmul(DNS[par][:, c * D:(c + 1) * D], ehT[par][:, i, c * P:(c + 1) * P],
                                           ewo[par][:, i, :], start=i == 0, stop=i == NI - 1)
            ins.then_inc(down_ps, 1)

        def act_expert(act, E, par):
            for u in range(2):
                act.wait_ge(up_ps, 2 * E + u + 1)
                if u == 0 and not (isinstance(E, int) and E < 2):
                    act.wait_ge(down_ps, E - 1)
                nc.scalar.activation(ehT[par][:, 2 * u:2 * u + 2, :].rearrange("p i c -> p (i c)"),
                                     UPS[par][u][:], ACT.Gelu).then_inc(gelu_done, 1)

        def dve_expert_in(dve, E, par):
            dve.wait_ge(ein_ps, E + 1)
            if not (isinstance(E, int) and E < 2):
                dve.wait_ge(up_ps, 2 * E - 2)
            nc.vector.tensor_scalar(einT[par][:], SC[0][par][:, 0:CAP], gcol[:], bcol[:],
                                    ALU.mult, ALU.add).then_inc(ein_ready, 1)

        def dve_expert_out(dve, E, par):
            dve.wait_ge(down_ps, E + 1)
            if not (isinstance(E, int) and E < 2):
                dve.wait_ge(eres_out[par], 8 * (E - par))
            nc.vector.tensor_copy(eres[par][:].rearrange("p c d -> p (c d)"), DNS[par][:, 0:2 * D]) \
                .then_inc(eres_ready, 1)

        def pool_expert_out(pool, E, e, par):
            pool.wait_ge(eres_ready, E + 1)
            nc.gpsimd.dma_start(eout[bass.ds(e * CAP, CAP), :].rearrange("(c p) d -> p c d", p=P), eres[par][:]) \
                .then_inc(eres_out[par], 16)

        HALF = NE // 2

        def pe_experts(pe, f):
            def two(k):
                for par in range(2):
                    pe_expert_in(pe, NE * f + 2 * k + par, par)
                    pe_expert_up(pe, NE * f + 2 * k + par, par)
                for par in range(2):
                    pe_expert_down(pe, NE * f + 2 * k + par, par)
            if f == 0:
                two(0)
            with pe.Fori(1 - f, HALF) as k:
                two(k)

        def expert_loop(eng, f, fn):
            if f == 0:
                fn(0)
            with eng.Fori(1 - f, HALF) as k:
                fn(k)

        xt = x.rearrange("b (t p) d -> p (b t) d", p=P)
        ot = out.rearrange("b (t p) d -> p (b t) d", p=P)

        EXTRA = {0: [("v", 0, 0)], 1: [("v", 1, 0)], 2: [("rank", 0, -2)], 3: [("o", 0, -1)],
                 4: [("v", 2, 0), ("yT", 0, 1)], 5: [("v", 3, 0)], 6: [("tT", 0, -1)], 7: [("logit", 0, -1)]}
        PJ_READ = {"g": (g_lo, NPAIR), "v": (v_ready, 4), "rank": (R[1]["seen_done"], 1), "o": (o_added, 1),
                   "yT": (yT_lo, 1), "tT": (R[1]["tT_ready"], 1), "logit": (R[1]["delta_ready"], 1)}

        def valid(b):
            return not isinstance(b, int) or 0 <= b < NB

        def at(b, p):
            return b * NPAIR + p

        def run(eng, batch):
            batch(0, 0)
            batch(1, 1)
            with eng.Fori(1, NB // 2 - 1) as k:
                batch(2 * k, 0)
                batch(2 * k + 1, 1)
            batch(NB - 2, 0)
            batch(NB - 1, 1)
            batch(NB, 0)
            batch(NB + 1, 1)

        def seq(b):
            return slice(BT * b, BT * b + BT) if isinstance(b, int) else bass.ds(BT * b, BT)

        def back(b, p, k):
            return (b, p - k) if p >= k else (b - 1, p - k + NPAIR)

        def fwd(b, p):
            return (b, p + 1) if p + 1 < NPAIR else (b + 1, 0)

        @block.sync
        def _(sp):
            for g in range(NG):
                sp.dma_start(X[:, g * GT:(g + 1) * GT, :], xt[:, g * GT:(g + 1) * GT, :]).then_inc(x_in[g], 16)
                if g == 0:
                    sp.dma_start(ident[:], ident_in).then_inc(const_in, 16)
                    sp.dma_start(tri_f[:], before_in).then_inc(const_in, 16)
                    sp.dma_start(ebase[:], ebase_in).then_inc(const_in, 16)
                    sp.dma_start(rev[:], rev_in).then_inc(const_in, 16)
                    sp.dma_start(noslot[:], noslot_in).then_inc(const_in, 16)
                    sp.dma_start(gcol[:], gamma).then_inc(const_in, 16)
                    sp.dma_start(bcol[:], beta).then_inc(const_in, 16)
                    sp.dma_start(gateT[:], gate).then_inc(const_in, 16)
            sp.wait_ge(zrow_set, 1)
            for q in range(4):
                sp.dma_start(disp[q * SLOTS // 4:(q + 1) * SLOTS // 4, :].rearrange("(p r) d -> p (r d)", p=P),
                             zrow[:]).then_inc(disp_zeroed, 16)
            sp.dma_start(wqT[:], w_qT.rearrange("(a p) d -> p a d", p=P)).then_inc(watt_in, 16)
            sp.dma_start(wkT[:], w_kT.rearrange("(a p) d -> p a d", p=P)).then_inc(watt_in, 16)
            sp.dma_start(wv[:], w_v).then_inc(watt_in, 16)
            sp.dma_start(wos[:], w_o.rearrange("(a p) d -> p a d", p=P)).then_inc(watt_in, 16)
            sp.wait_ge(R[0]["scattered"], NT * 16)
            expert_loop(sp, 0, lambda k: [sp_expert(sp, 2 * k + j, 2 * k + j, j) for j in range(2)])
            sp.wait_ge(R[1]["scattered"], NT * 16)
            expert_loop(sp, 1, lambda k: [sp_expert(sp, NE + 2 * k + j, 2 * k + j, j) for j in range(2)])

            def store(b, par):
                sp.wait_ge(comb2, BT * b + BT)
                sp.dma_start(ot[:, seq(b), :], res[par][:]).then_inc(out_sent[par], 16)
            with sp.Fori(0, NB // 2) as k:
                for par in range(2):
                    store(2 * k + par, par)
            for par in range(2):
                sp.wait_ge(out_sent[par], NB * 8)

        @block.gpsimd
        def _(pool):
            nc.gpsimd.memset(zrow[:], 0.0).then_inc(zrow_set, 1)
            nc.gpsimd.memset(mhalf[:], -0.5).then_inc(consts, 1)
            nc.gpsimd.memset(epsc[:], EPS).then_inc(consts, 1)
            nc.gpsimd.memset(ones[:], 1.0).then_inc(consts, 1)
            nc.gpsimd.memset(rt[0].seen[:], 0.0).then_inc(consts, 1)
            nc.gpsimd.memset(rt[1].seen[:], 0.0).then_inc(consts, 1)
            pool.wait_ge(consts, 5)
            pool.wait_ge(disp_zeroed, 64)

            def group(g):
                route_rstd(pool, 0, g)
                pool.wait_ge(R[0]["dest_ready"], g + 1)
                route_scatter(pool, 0)
            for g in range(NG):
                group(g)
            pool.wait_ge(wv_hi, 1)
            nc.gpsimd.tensor_tensor(wvl[:], wv[:], wvh[:].bitcast(F32), ALU.subtract).then_inc(wv_lo, 1)
            for e in range(NE):
                pool_expert_out(pool, e, e, e % 2)
            for par in range(2):
                pool.wait_ge(eres_out[par], 8 * NE)

            def gather(b, par):
                for j in range(BT):
                    nc.gpsimd.indirect_dma_start(
                        out=got[par][:, j, :], out_offset=None, in_=eout[:, :],
                        in_offset=bass.IndirectOffsetOnAxis(gidx[par][:, j:j + 1], 0)).then_inc(got_in[par], 16)

            def prep_rstd(b):
                pool.wait_ge(c_var, b + 1)
                nc.gpsimd.tensor_tensor(c_rs[:], c_vare[:], mhalf[:, 0:BT], ALU.pow).then_inc(c_rstd, 1)

            def batch(b, par):
                for p in range(NPAIR):
                    pb, pp = back(b, p, 1)
                    if p == 0 and valid(b + 1):
                        pool.wait_ge(idx_ready, b + 2)
                    if p == 4 and valid(b - 2):
                        pool.wait_ge(R[1]["dest_ready"], b - 1)
                    if valid(pb):
                        pool.wait_ge(rsum_ready, at(pb, pp) + 1)
                        q = pp % 4
                        v = prob[q][:].rearrange("p c h k -> p (c h) k")
                        nc.gpsimd.tensor_tensor(v, v, bc(rsum[q][:], SEQ), ALU.mult).then_inc(prob_ready, 1)
                    if p == 0 and valid(b + 1):
                        gather(b + 1, 1 - par)
                    if p == 2 and valid(b + 1):
                        prep_rstd(b + 1)
                    if p == 4 and valid(b - 2):
                        route_scatter(pool, 1)
                    if p == 4 and valid(b - 1):
                        route_rstd(pool, 1, b - 1)
            pool.wait_ge(idx_ready, 1)
            gather(0, 0)
            prep_rstd(0)
            run(pool, batch)
            for e in range(NE):
                pool_expert_out(pool, NE + e, e, e % 2)
            for par in range(2):
                pool.wait_ge(eres_out[par], 16 * NE)

            def gather2(b, par):
                pool.wait_ge(gi2, b + 1)
                for j in range(BT):
                    nc.gpsimd.indirect_dma_start(
                        out=got[par][:, j, :], out_offset=None, in_=eout[:, :],
                        in_offset=bass.IndirectOffsetOnAxis(gidx[par][:, j:j + 1], 0)).then_inc(got2[par], 16)
            for b in range(NB):
                gather2(b, b % 2)

        @block.scalar
        def _(act):
            act.wait_ge(watt_in, 64)
            nc.scalar.activation(wvh[:], wv[:], ACT.Copy).then_inc(wv_hi, 1)
            for q in range(4):
                act.wait_ge(a_ps, q + 1)
                nc.scalar.activation(heads4(ah, q), four(ABANK[q]), ACT.Copy).then_inc(a_hi, 1)
            act.wait_ge(consts, 5)
            act.wait_ge(const_in, 128)

            def route_tT(f, i, banks, width):
                r, s = rt[f], R[f]
                for k, bank in enumerate(banks):
                    act.wait_ge(s["tT_ps"], len(banks) * i + k + 1)
                    nc.scalar.activation(r.tokT[:].rearrange("p n q -> p (n q)")[:, k * width:(k + 1) * width],
                                         bank[:, 0:width], ACT.Identity, bias=bcol[:], scale=gcol[:]) \
                        .then_inc(s["tT_ready"], 1)

            def route_exp(f, i):
                r, s = rt[f], R[f]
                act.wait_ge(s["delta_ready"], i + 1)
                nc.scalar.activation(r.exl[:], r.dlt[:], ACT.Exp).then_inc(s["exl_ready"], 1)

            with act.Fori(0, NG) as g:
                route_tT(0, g, [SC[0][0], SC[0][1]], 512)
                route_exp(0, g)
            expert_loop(act, 0, lambda k: [act_expert(act, 2 * k + j, j) for j in range(2)])

            def prep_hi(b, par):
                act.wait_ge(yT_ps, b + 1)
                nc.scalar.activation(yTh[par][:], PJ[:, 0:SEQ], ACT.Copy).then_inc(yT_hi, 1)

            def g_hi_part(b, p):
                act.wait_ge(g_ps, at(b, p) + 1)
                if not (isinstance(b, int) and at(b, p) < 2):
                    act.wait_ge(scores_ps, 2 * at(b, p) - 2)
                nc.scalar.activation(Gh[p % 2][:], PJ[:], ACT.Copy).then_inc(g_hi, 1)

            def batch(b, par):
                for p in range(NPAIR):
                    nb, np_ = fwd(b, p)
                    if valid(nb):
                        g_hi_part(nb, np_)
                    pb, pp = back(b, p, 1)
                    if valid(pb):
                        act.wait_ge(bias_ready, at(pb, pp) + 1)
                        if not (isinstance(pb, int) and at(pb, pp) < 4):
                            act.wait_ge(pT_ps, 2 * at(pb, pp) - 6)
                        for c in range(2):
                            for h in range(2):
                                k = 2 * c + h
                                ins = nc.scalar.activation(
                                    prob[pp % 4][:, c, h, :], SC[pp % 2][c][:, h * SEQ:(h + 1) * SEQ], ACT.Exp,
                                    bias=nbias[pp % 4][:, k:k + 1], scale=SCALE, accum_out=sums[pp % 4][:, k:k + 1])
                            ins.then_inc(exp_done, 1)
                    tb, tp = back(b, p, 2)
                    if valid(tb):
                        act.wait_ge(pT_ps, 2 * at(tb, tp) + 1)
                        if not (isinstance(tb, int) and at(tb, tp) < 2):
                            act.wait_ge(z_ps, at(tb, tp) - 1)
                        nc.scalar.activation(probT[tp % 2][0][:].rearrange("p j q -> p (j q)"), PT[0][:],
                                             ACT.Copy).then_inc(pT_even, 1)
                    zb, zp = back(b, p, 3)
                    if valid(zb):
                        act.wait_ge(z_ps, at(zb, zp) + 1)
                        zpar = par if p >= 3 else 1 - par
                        if not (isinstance(zb, int) and zb < 2):
                            act.wait_ge(o_ps, zb - 1)
                        nc.scalar.activation(zT[zpar][:, zp, :], Z[:, 0:SEQ], ACT.Copy).then_inc(z_ready, 1)
                    for kind, u, db in EXTRA[p]:
                        tb = b + db
                        if not valid(tb):
                            continue
                        if kind == "v":
                            act.wait_ge(v_ps, 4 * tb + u + 1)
                            nc.scalar.activation(V[:, u % 2, (u // 2) * 512:(u // 2 + 1) * 512], PJ[:],
                                                 ACT.Copy).then_inc(v_ready, 1)
                        elif kind == "yT":
                            prep_hi(tb, 1 - par)
                        elif kind == "tT":
                            route_tT(1, tb, [PJ], SEQ)
                    if p == 0 and valid(b - 2):
                        route_exp(1, b - 2)
            prep_hi(0, 0)
            g_hi_part(0, 0)
            run(act, batch)
            expert_loop(act, 1, lambda k: [act_expert(act, NE + 2 * k + j, j) for j in range(2)])

        @block.vector
        def _(dve):
            dve.wait_ge(const_in, 128)
            nc.vector.tensor_copy(before[:], tri_f[:]).then_inc(before_ready, 1)

            def group(g, gi):
                xs = X[:, gi, :]
                route_stats(dve, 0, g, xs)
                route_norm(dve, 0, g, xs, xs)
                route_pick(dve, 0, g, PJ[:, 0:GT * NE].rearrange("p (n e) -> p n e", e=NE))
                route_final(dve, 0, g, Z[:, 0:(GT + 1) * NE].rearrange("p (n e) -> p n e", e=NE), gi)
            for g in range(NG):
                dve.wait_ge(x_in[g], 16)
            for q in range(4):
                dve.wait_ge(a_hi, q + 1)
                nc.vector.tensor_tensor(heads4(al, q), four(ABANK[q]), heads4(ah, q).bitcast(F32),
                                        ALU.subtract).then_inc(a_lo, 1)
            group(0, slice(0, GT))
            with dve.Fori(1, NG) as g:
                group(g, bass.ds(g * GT, GT))

            def experts(f):
                def two(k):
                    dve_expert_in(dve, NE * f + 2 * k, 0)
                    dve_expert_in(dve, NE * f + 2 * k + 1, 1)
                    dve_expert_out(dve, NE * f + 2 * k, 0)
                    dve_expert_out(dve, NE * f + 2 * k + 1, 1)
                expert_loop(dve, f, two)
            experts(0)

            def fetch_idx(b, par):
                nc.vector.tensor_copy(gidx[par][:], rt[0].src[:, seq(b)]).then_inc(idx_ready, 1)

            def prep_combine(b, par):
                dve.wait_ge(got_in[par], 8 * BT * (b - par) + 16 * BT)
                for j in range(BT):
                    t = slice(BT * b + j, BT * b + j + 1) if isinstance(b, int) else bass.ds(BT * b + j, 1)
                    ins = nc.vector.scalar_tensor_tensor(x1[:, j:j + 1, :], got[par][:, j:j + 1, :],
                                                         rt[0].wt[:, t], X[:, t, :], ALU.mult, ALU.add)
                ins.then_inc(combined, 1)
                dve.wait_ge(combined, b + 1)
                for j in range(BT):
                    ins = nc.vector.bn_stats(c_st[:, j, :], x1[:, j, :])
                ins.then_inc(c_stats, 1)
                dve.wait_ge(c_stats, b + 1)
                dve_var(dve, c_st, c_chain, c_mean[:], c_diff[:], c_m2[:], c_vare[:], c_varr[:],
                        b * N_STATS, c_var)

            def prep_norm(b):
                dve.wait_ge(c_rstd, b + 1)
                if not (isinstance(b, int) and b == 0):
                    dve.wait_ge(yT_ps, b)
                for j in range(BT):
                    ins = nc.vector.tensor_scalar(ya[:, j:j + 1, :], x1[:, j:j + 1, :], c_mean[:, j:j + 1],
                                                  c_rs[:, j:j + 1], ALU.subtract, ALU.mult)
                ins.then_inc(ya_ready, 1)
                dve.wait_ge(ya_ready, b + 1)
                nc.vector.tensor_tensor(X[:, seq(b), :], x1[:], ya[:], ALU.add).then_inc(x_plus_ya, 1)

            def prep_lo(b, par):
                dve.wait_ge(yT_hi, b + 1)
                nc.vector.tensor_tensor(yTl[par][:], PJ[:, 0:SEQ], yTh[par][:].bitcast(F32),
                                        ALU.subtract).then_inc(yT_lo, 1)

            def g_lo_part(b, p):
                dve.wait_ge(g_hi, at(b, p) + 1)
                nc.vector.tensor_tensor(Gl[p % 2][:], PJ[:], Gh[p % 2][:].bitcast(F32), ALU.subtract) \
                    .then_inc(g_lo, 1)

            def batch(b, par):
                for p in range(NPAIR):
                    nb, np_ = fwd(b, p)
                    if valid(nb):
                        g_lo_part(nb, np_)
                    pb, pp = back(b, p, 1)
                    if valid(pb):
                        dve.wait_ge(exp_done, 2 * at(pb, pp) + 2)
                        if not (isinstance(pb, int) and at(pb, pp) < 4):
                            dve.wait_ge(prob_ready, at(pb, pp) - 3)
                        nc.vector.reciprocal(rsum[pp % 4][:], sums[pp % 4][:]).then_inc(rsum_ready, 1)
                    if valid(b):
                        g = at(b, p)
                        for c in range(2):
                            dve.wait_ge(scores_ps, 2 * g + c + 1)
                            ins = nc.vector.tensor_reduce(
                                mx[p % 4][:, 2 * c:2 * c + 2],
                                SC[p % 2][c][:].rearrange("p (h k) -> p h k", h=2), AX.X, ALU.max)
                        ins.then_inc(max_done, 1)
                        dve.wait_ge(max_done, g + 1)
                        nc.vector.tensor_scalar(nbias[p % 4][:], mx[p % 4][:], -SCALE, None,
                                                ALU.mult).then_inc(bias_ready, 1)
                    tb, tp = back(b, p, 2)
                    if valid(tb):
                        dve.wait_ge(pT_ps, 2 * at(tb, tp) + 2)
                        if not (isinstance(tb, int) and at(tb, tp) < 2):
                            dve.wait_ge(z_ps, at(tb, tp) - 1)
                        nc.vector.tensor_copy(probT[tp % 2][1][:].rearrange("p j q -> p (j q)"),
                                              PT[1][:]).then_inc(pT_odd, 1)
                    if p == 0 and valid(b + 1):
                        fetch_idx(b + 1, 1 - par)
                    if p == 7 and valid(b - 1):
                        route_pick(dve, 1, b - 1, PJ[:, 0:BT * NE].rearrange("p (n e) -> p n e", e=NE))
                    if p == 1 and valid(b + 1):
                        prep_combine(b + 1, 1 - par)
                    if p == 3 and valid(b + 1):
                        prep_norm(b + 1)
                    if p == 2 and valid(b - 2):
                        route_final(dve, 1, b - 2, PJ[:, 0:(BT + 1) * NE].rearrange("p (n e) -> p n e", e=NE),
                                    seq(b - 2))
                    if p == 3 and valid(b - 1):
                        dve.wait_ge(o_ps, b)
                        nc.vector.tensor_tensor(x2[:], PJ[:, 0:BT * D]
                                                .rearrange("p (t d) -> p t d", d=D), X[:, seq(b - 1), :],
                                                ALU.add).then_inc(o_added, 1)
                        dve.wait_ge(o_added, b)
                        route_stats(dve, 1, b - 1, x2)
                    if p == 4 and valid(b + 1):
                        prep_lo(b + 1, 1 - par)
                    if p == 5 and valid(b - 1):
                        route_norm(dve, 1, b - 1, x2, X[:, seq(b - 1), :])
            fetch_idx(0, 0)
            prep_combine(0, 0)
            prep_norm(0)
            prep_lo(0, 0)
            g_lo_part(0, 0)
            run(dve, batch)
            experts(1)

            def combine2(b, par):
                dve.wait_ge(got2[par], 8 * BT * (b - par) + 16 * BT)
                if not (isinstance(b, int) and b < 2):
                    dve.wait_ge(out_sent[par], 8 * (b - par))
                for j in range(BT):
                    t = slice(BT * b + j, BT * b + j + 1) if isinstance(b, int) else bass.ds(BT * b + j, 1)
                    nc.vector.scalar_tensor_tensor(res[par][:, j:j + 1, :], got[par][:, j:j + 1, :], rt[1].wt[:, t],
                                                   X[:, t, :], ALU.mult, ALU.add).then_inc(comb2, 1)

            def fetch2(b, par):
                nc.vector.tensor_copy(gidx[par][:], rt[1].src[:, seq(b)]).then_inc(gi2, 1)
            for par in range(2):
                fetch2(par, par)
            for par in range(2):
                combine2(par, par)
            with dve.Fori(1, NB // 2) as k:
                for par in range(2):
                    fetch2(2 * k + par, par)
                for par in range(2):
                    combine2(2 * k + par, par)

        @block.tensor
        def _(pe):
            pe.wait_ge(watt_in, 64)
            for q in range(4):
                bank = ABANK[q]
                for k in range(4):
                    h = 8 * (q // 2) + 2 * k + q % 2
                    r = slice(DK * (h % 2), DK * (h % 2) + DK)
                    ins = nc.tensor.matmul(bank[:, k * D:(k + 1) * D], wqT[r, h // 2, :], wkT[r, h // 2, :],
                                           start=True, stop=True)
                ins.then_inc(a_ps, 1)
            pe.wait_ge(const_in, 128)
            pe.wait_ge(consts, 5)
            pe.wait_ge(before_ready, 1)

            def route_group(g, first):
                r, s = rt[0], R[0]
                pe.wait_ge(s["tok_done"], g + 1)
                if not first:
                    pe.wait_ge(s["tT_ready"], 2 * g)
                for j in range(GT):
                    ins = nc.tensor.transpose(SC[0][j // 4][:, (j % 4) * P:(j % 4 + 1) * P], r.tok[:, j, :], ident[:])
                    if j % 4 == 3:
                        ins.then_inc(s["tT_ps"], 1)
                pe.wait_ge(s["tT_ready"], 2 * g + 2)
                if not first:
                    pe.wait_ge(s["delta_ready"], g)
                for j in range(GT):
                    ins = nc.tensor.matmul(PJ[:, j * NE:(j + 1) * NE], r.tokT[:, j, :], gateT[:], start=True, stop=True)
                ins.then_inc(s["logit_ps"], 1)
                pe.wait_ge(s["hot_ready"], g + 1)
                if not first:
                    pe.wait_ge(s["seen_done"], g)
                pe_ranks(0, Z[:, 0:(GT + 1) * NE].rearrange("p (n e) -> p n e", e=NE)).then_inc(s["rank_ps"], 1)
            route_group(0, True)
            with pe.Fori(1, NG) as g:
                route_group(g, False)
            pe.wait_ge(a_lo, 4)
            pe.wait_ge(R[0]["seen_done"], NG)
            pe_experts(pe, 0)
            pe.wait_ge(eres_ready, NE)
            pe.wait_ge(wv_lo, 1)

            last = [None]

            def take(b, kind, u, db):
                if last[0] is not None:
                    k, lu, ldb = last[0]
                    s, per = PJ_READ[k]
                    pe.wait_ge(s, per * (b + ldb) + lu + 1)
                last[0] = (kind, u, db)

            def pe_yT(b, par):
                pe.wait_ge(ya_ready, b + 1)
                for j in range(BT):
                    ins = nc.tensor.transpose(PJ[:, j * P:(j + 1) * P], ya[:, j, :], ident[:])
                ins.then_inc(yT_ps, 1)

            def pe_g(b, p, par):
                if p == 0:
                    pe.wait_ge(yT_lo, b + 1)
                for h in range(2):
                    hh = 2 * p + h
                    o = PJ[:, h * SEQ:(h + 1) * SEQ]
                    nc.tensor.matmul(o, ah[:, hh, :], yTh[par][:], start=True, stop=False)
                    nc.tensor.matmul(o, al[:, hh, :], yTh[par][:], start=False, stop=False)
                    ins = nc.tensor.matmul(o, ah[:, hh, :], yTl[par][:], start=False, stop=True)
                ins.then_inc(g_ps, 1)

            def batch(b, par):
                for p in range(NPAIR):
                    nb, np_ = fwd(b, p)
                    if valid(nb):
                        take(b, "g", np_, 0 if p + 1 < NPAIR else 1)
                        pe_g(nb, np_, par if p + 1 < NPAIR else 1 - par)
                    if valid(b):
                        g = at(b, p)
                        pe.wait_ge(g_lo, g + 1)
                        if not (isinstance(b, int) and g < 2):
                            pe.wait_ge(exp_done, 2 * g - 2)
                        for c in range(2):
                            for h in range(2):
                                o = SC[p % 2][c][:, h * SEQ:(h + 1) * SEQ]
                                q = slice(h * SEQ + c * P, h * SEQ + (c + 1) * P)
                                nc.tensor.matmul(o, Gh[p % 2][:, q], yTh[par][:], start=True, stop=False)
                                nc.tensor.matmul(o, Gh[p % 2][:, q], yTl[par][:], start=False, stop=False)
                                ins = nc.tensor.matmul(o, Gl[p % 2][:, q], yTh[par][:], start=False, stop=True)
                            ins.then_inc(scores_ps, 1)
                    tb, tp = back(b, p, 2)
                    if valid(tb):
                        g = at(tb, tp)
                        pe.wait_ge(prob_ready, g + 1)
                        for h in range(2):
                            if not (isinstance(tb, int) and g < 1):
                                pe.wait_ge([pT_even, pT_odd][h], g)
                            for j in range(2):
                                for c in range(2):
                                    ins = nc.tensor.transpose(
                                        PT[h][:, j * SEQ + c * P:j * SEQ + (c + 1) * P],
                                        prob[tp % 4][:, c, h, j * P:(j + 1) * P], ident[:])
                            ins.then_inc(pT_ps, 1)
                    zb, zp = back(b, p, 3)
                    if valid(zb):
                        g = at(zb, zp)
                        pe.wait_ge(pT_even, g + 1)
                        pe.wait_ge(pT_odd, g + 1)
                        pe.wait_ge(v_ready, 4 * zb + (2 if zp < 4 else 4))
                        if not (isinstance(zb, int) and g < 1):
                            pe.wait_ge(z_ready, g)
                        for j in range(2):
                            for h in range(2):
                                ins = nc.tensor.matmul(
                                    Z[DK * h:DK * h + DK, 0:SEQ], V[:, j, (2 * zp + h) * DK:(2 * zp + h + 1) * DK],
                                    probT[zp % 2][h][:, j, :], start=j == 0, stop=j == 1)
                        ins.then_inc(z_ps, 1)
                    for kind, u, db in EXTRA[p]:
                        tb = b + db
                        if not valid(tb):
                            continue
                        if kind == "v":
                            take(b, kind, u, db)
                            half = slice((u // 2) * 512, (u // 2 + 1) * 512)
                            t = slice((u % 2) * P, (u % 2 + 1) * P)
                            nc.tensor.matmul(PJ[:], yTh[par][:, t], wvh[:, half], start=True, stop=False)
                            nc.tensor.matmul(PJ[:], yTh[par][:, t], wvl[:, half], start=False, stop=False)
                            nc.tensor.matmul(PJ[:], yTl[par][:, t], wvh[:, half], start=False,
                                             stop=True).then_inc(v_ps, 1)
                        elif kind == "yT":
                            take(b, kind, u, db)
                            pe_yT(tb, 1 - par)
                        elif kind == "o":
                            pe.wait_ge(z_ready, at(tb, NPAIR - 1) + 1)
                            take(b, kind, u, db)
                            for c in range(BT):
                                for k in range(NPAIR):
                                    ins = nc.tensor.matmul(PJ[:, c * D:(c + 1) * D],
                                                           zT[1 - par][:, k, c * P:(c + 1) * P], wos[:, k, :],
                                                           start=k == 0, stop=k == NPAIR - 1)
                            ins.then_inc(o_ps, 1)
                        elif kind == "tT":
                            pe.wait_ge(R[1]["tok_done"], tb + 1)
                            take(b, kind, u, db)
                            for j in range(BT):
                                ins = nc.tensor.transpose(PJ[:, j * P:(j + 1) * P], rt[1].tok[:, j, :], ident[:])
                            ins.then_inc(R[1]["tT_ps"], 1)
                        elif kind == "logit":
                            pe.wait_ge(R[1]["tT_ready"], tb + 1)
                            take(b, kind, u, db)
                            for j in range(BT):
                                ins = nc.tensor.matmul(PJ[:, j * NE:(j + 1) * NE], rt[1].tokT[:, j, :], gateT[:],
                                                       start=True, stop=True)
                            ins.then_inc(R[1]["logit_ps"], 1)
                        elif kind == "rank":
                            pe.wait_ge(R[1]["hot_ready"], tb + 1)
                            take(b, kind, u, db)
                            pe_ranks(1, PJ[:, 0:(BT + 1) * NE].rearrange("p (n e) -> p n e", e=NE)) \
                                .then_inc(R[1]["rank_ps"], 1)
                k, u, db = last[0]
                last[0] = (k, u, db - 1)
            take(0, "yT", 0, 0)
            pe_yT(0, 0)
            take(0, "g", 0, 0)
            pe_g(0, 0, 0)
            run(pe, batch)
            pe.wait_ge(R[1]["seen_done"], NB)
            pe_experts(pe, 1)


_INS = ["x", "w_qT", "w_kT", "w_v", "w_o", "gate", "gamma", "beta", "wi", "wo", "ident", "before", "ebase", "rev",
        "noslot"]


def kernel(**inputs):
    from concourse import bacc as _bacc
    from concourse.bass_utils import run_bass_kernel_spmd as _run

    a = {k: np.asarray(v) for k, v in inputs.items()}
    p = np.arange(P)
    data = {
        "x": a["L0_attn_x"],
        "w_qT": a["L0_attn_w_q"].transpose(0, 2, 1).reshape(NH * DK, D),
        "w_kT": a["L0_attn_w_k"].transpose(0, 2, 1).reshape(NH * DK, D),
        "w_v": a["L0_attn_w_v"].transpose(1, 0, 2).reshape(D, NH * DK),
        "w_o": a["L0_attn_w_o"],
        "gate": a["L0_ffn_gate_weight"].T,
        "gamma": a["L0_ffn_ln_gamma"].reshape(D, 1),
        "beta": a["L0_ffn_ln_beta"].reshape(D, 1),
        "wi": a["L0_ffn_wi"],
        "wo": a["L0_ffn_wo"],
        "ident": np.eye(P, dtype=np.float32),
        "before": np.triu(np.ones((P, P), np.float32), 1),
        "ebase": np.tile(np.arange(NE, dtype=np.float32) * CAP, (P, 1)),
        "rev": np.tile(np.arange(NE, 0, -1, dtype=np.float32), (P, 1)),
        "noslot": (NOSLOT + np.arange(GT)[None, :] * P + p[:, None]).astype(np.float32),
    }
    nc = _bacc.Bacc("TRN2", target_bir_lowering=False, num_devices=1)
    arrays, args = {}, []
    for name in _INS:
        v = np.ascontiguousarray(data[name])
        arrays[f"in_{name}_dram"] = v
        args.append(nc.dram_tensor(f"in_{name}_dram", v.shape, mybir.dt.from_np(v.dtype), kind="ExternalInput").ap())
    out = nc.dram_tensor("out_0_dram", (NB, SEQ, D), F32, kind="ExternalOutput").ap()
    macaron_kernel(nc, *args, out)
    r = _run(nc, [arrays], core_ids=[0])
    return r.results[0]["out_0_dram"]
```

```python
import numpy as np
import concourse.bass as bass
from concourse import mybir
from contextlib import ExitStack

F32 = mybir.dt.float32
F32R = mybir.dt.float32r
BF16 = mybir.dt.bfloat16
I32 = mybir.dt.int32
ALU = mybir.AluOpType
ACT = mybir.ActivationFunctionType
AX = mybir.AxisListType

P = 128
D = 128
NB, SEQ = 16, 256
NT = NB * SEQ // P
NH, DK = 16, 64
NPAIR = NH // 2
NE, FF = 8, 512
CAP = 256
SLOTS = NE * CAP
NI = FF // P
GT = 8
NG = NT // GT
BT = SEQ // P
EPS = 1e-5
SCALE = 1.0 / float(np.sqrt(DK))
NOSLOT = 2 * SLOTS


ROW_RES, ROW_ID, ROW_WT, ROW = D, 2 * D, 2 * D + 1, 2 * D + 2
NOTOK = 2 * NT * P


def macaron_kernel(nc, x, w_qT, w_kT, w_v, w_o, gate, gamma, beta, wi, wo, ident_in, before_in, ebase_in, rev_in,
                   noslot_in, tokid_in, empty_in, out):
    ctx = ExitStack()
    with ctx:
        def sb(name, shape, dt=F32):
            return ctx.enter_context(nc.sbuf_tensor(name, shape, dt))

        def sem(name):
            return ctx.enter_context(nc.semaphore(name))

        X = sb("X", [P, NT, D])
        ident = sb("ident", [P, P])
        before = sb("before", [P, P], BF16)
        ones = sb("ones", [P, P], BF16)
        tri_f = sb("tri_f", [P, P])
        ebase = sb("ebase", [P, NE])
        rev = sb("rev", [P, NE])
        noslot = sb("noslot", [P, GT])
        gcol = sb("gcol", [P, 1])
        bcol = sb("bcol", [P, 1])
        gateT = sb("gateT", [P, NE])
        mhalf = sb("mhalf", [P, 2 * GT])
        wqT = sb("wqT", [P, NPAIR, D])
        wkT = sb("wkT", [P, NPAIR, D])
        wv = sb("wv", [P, NH * DK])
        wvh = sb("wvh", [P, NH * DK], F32R)
        wvl = sb("wvl", [P, NH * DK], F32R)
        wos = sb("wos", [P, NPAIR, D])
        ah = sb("ah", [P, NH, D], F32R)
        al = sb("al", [P, NH, D], F32R)
        shared = [sb(f"shared{q}", [P, GT * ROW]) for q in range(NG)]

        class Routing:
            def __init__(self, f, n, ring):
                self.n, self.ring = n, ring
                small = ("mean", "diff", "m2", "var", "rvar", "ratio", "rst", "amul", "lmax",
                         "cmax", "rank", "base", "keep", "den", "rden", "d1", "d2", "d3")
                wide = ("dlt", "exl", "cand", "hotf", "lg", "rkp", "rk", "rsel", "bsel")
                self.tiles = {k: [sb(f"r{f}_{k}{q}", [P, n]) for q in range(ring)] for k in small}
                for k in wide:
                    self.tiles[k] = [sb(f"r{f}_{k}{q}", [P, n, NE]) for q in range(ring)]
                self.tiles["vars"] = [sb(f"r{f}_vars{q}", [P, 2 * n]) for q in range(ring)]
                self.tiles["rstd"] = [sb(f"r{f}_rstd{q}", [P, 2 * n]) for q in range(ring)]
                self.tiles["st"] = [sb(f"r{f}_st{q}", [P, n, 6]) for q in range(ring)]
                self.tiles["cadd"] = [sb(f"r{f}_cadd{q}", [P, n]) for q in range(ring)]
                self.tiles["tot"] = [sb(f"r{f}_tot{q}", [P, NE]) for q in range(ring)]
                self.tiles["hot"] = [sb(f"r{f}_hot{q}", [P, n, NE], BF16) for q in range(ring)]
                self.tiles["dest"] = [sb(f"r{f}_dest{q}", [P, n], I32) for q in range(ring)]
                self.tiles["tokT"] = [sb(f"r{f}_tokT{q}", [P, n, P]) for q in range(1)] * ring
                self.tiles["row"] = ([t[:].rearrange("p (n r) -> p n r", r=ROW) for t in shared] if f == 0 else
                                     [sb(f"r{f}_row{q}", [P, n, ROW]) for q in range(ring)])
                self.seen = sb(f"r{f}_seen", [P, NE])

            def __call__(self, name, i):
                return self.tiles[name][i if self.ring > 1 else 0]
        rt = [Routing(0, GT, NG), Routing(1, BT, 1)]
        tokid = sb("tokid", [P, NT])
        empty = sb("empty", [P, 4, ROW])
        ewi = [X[:, e * NI:(e + 1) * NI, :].rearrange("p i j -> p (i j)") for e in range(NE)]
        ewi_hi = [sb(f"ewi_hi{e}", [P, FF], F32R) for e in range(NE)]
        ewi_lo = [sb(f"ewi_lo{e}", [P, FF], F32R) for e in range(NE)]
        ewo = [sb(f"ewo{e}", [P, NI, D]) for e in range(NE)]
        ein = [sb(f"ein{i}", [P, 2, ROW]) for i in range(4)]
        einT = sb("einT", [P, CAP])
        eTh = [sb(f"eTh{i}", [P, CAP], F32R) for i in range(2)]
        eTl = [sb(f"eTl{i}", [P, CAP], F32R) for i in range(2)]
        ehT = [sb(f"ehT{i}", [P, NI, CAP]) for i in range(2)]
        eid = [sb(f"eid{i}", [P, 2], I32) for i in range(2)]
        eres = [sb(f"eres{i}", [P, 2, D]) for i in range(2)]
        c_st = sb("c_st", [P, BT, 6])
        c_mean, c_diff, c_m2, c_var_, c_vare, c_rs, c_mul, c_add = [
            sb(f"c_{k}", [P, BT]) for k in ("mean", "diff", "m2", "var", "vare", "rs", "mul", "add")]
        ya = sb("ya", [P, BT, D])
        x1 = [sb(f"x1{i}", [P, BT, D]) for i in range(2)]
        x1y = [sb(f"x1y{i}", [P, BT, D]) for i in range(2)]
        x2 = sb("x2", [P, BT, D])
        yTh = [sb(f"yTh{i}", [P, SEQ], F32R) for i in range(2)]
        yTl = [sb(f"yTl{i}", [P, SEQ], F32R) for i in range(2)]
        Gh = [sb(f"Gh{i}", [P, 2 * SEQ], F32R) for i in range(2)]
        Gl = [sb(f"Gl{i}", [P, 2 * SEQ], F32R) for i in range(2)]
        V = X[:, 0:16, :].rearrange("p (t c) d -> p t (c d)", t=BT)
        mx = [sb(f"mx{i}", [P, 4]) for i in range(4)]
        nbias = [sb(f"nbias{i}", [P, 4]) for i in range(4)]
        sums = [sb(f"sums{i}", [P, 4]) for i in range(4)]
        rsum = [sb(f"rsum{i}", [P, 4]) for i in range(4)]
        prob = [shared[i // 2][:, (i % 2) * 4 * SEQ:(i % 2 + 1) * 4 * SEQ]
                .rearrange("p (c h k) -> p c h k", c=2, h=2) for i in range(4)]
        probT = [[X[:, 16 + 8 * i + 4 * h:20 + 8 * i + 4 * h, :].rearrange("p (j c) d -> p j (c d)", j=2)
                  for h in range(2)] for i in range(2)]
        zT = [shared[2 + i][:, 0:NPAIR * SEQ].rearrange("p (k q) -> p k q", k=NPAIR) for i in range(2)]
        SC = [[ctx.enter_context(nc.psum_tensor(f"SC{i}{c}", [P, 512], F32)) for c in range(2)] for i in range(2)]
        PT = [ctx.enter_context(nc.psum_tensor(f"PT{h}", [P, 512], F32)) for h in range(2)]
        PJ = ctx.enter_context(nc.psum_tensor("PJ", [P, 512], F32))
        Z = ctx.enter_context(nc.psum_tensor("Z", [P, 512], F32))
        disp = [nc.dram_tensor(f"disp{f}", [SLOTS, ROW], F32, kind="Internal").ap() for f in range(2)]
        x1_dram = nc.dram_tensor("x1_dram", [NT * P, D], F32, kind="Internal").ap()

        x_in = [sem(f"x_in{g}") for g in range(NG)]
        const_in, watt_in, consts = sem("const_in"), sem("watt_in"), sem("consts")
        before_ready, empty_in_done = sem("before_ready"), sem("empty_in_done")
        disp_emptied = [sem(f"disp_emptied{f}") for f in range(2)]
        a_ps, a_hi, a_lo, wv_hi, wv_lo = sem("a_ps"), sem("a_hi"), sem("a_lo"), sem("wv_hi"), sem("wv_lo")
        R = []
        for f in range(2):
            R.append({k: sem(f"f{f}_{k}") for k in (
                "stats", "var_ready", "rstd_ready", "norm", "y_done", "tok_done", "tT_ps", "tT_ready", "logit_ps",
                "delta_ready", "exl_ready", "hot_ready", "hots", "rank_ps", "seen_done", "final", "dest_ready",
                "scattered", "first", "x_done", "stored", "logit_read", "rank_read", "aff", "id_set")})
        ein_in, ein_ps, ein_ready = [sem(f"ein_in{i}") for i in range(4)], sem("ein_ps"), sem("ein_ready")
        ew_in = [sem(f"ew_in{e}") for e in range(NE)]
        up_ps, gelu_done, down_ps, eres_ready = sem("up_ps"), sem("gelu_done"), sem("down_ps"), sem("eres_ready")
        eres_out = [sem(f"eres_out{i}") for i in range(2)]
        x1_in = [sem(f"x1_in{i}") for i in range(2)]
        ein_read, ein_hi, ewi_rounded, ewi_split = [sem(k) for k in ("ein_read", "ein_hi", "ewi_rounded", "ewi_split")]
        eid_ready, c_aff = sem("eid_ready"), sem("c_aff")
        c_stats, c_rstd, c_chain = sem("c_stats"), sem("c_rstd"), sem("c_chain")
        ya_ready, x_plus_ya = sem("ya_ready"), sem("x_plus_ya")
        yT_ps, yT_hi, yT_lo = sem("yT_ps"), sem("yT_hi"), sem("yT_lo")
        g_ps, g_hi, g_lo = sem("g_ps"), sem("g_hi"), sem("g_lo")
        v_ps, v_ready = sem("v_ps"), sem("v_ready")
        scores_ps, max_done, bias_ready = sem("scores_ps"), sem("max_done"), sem("bias_ready")
        exp_done, rsum_ready, prob_ready = sem("exp_done"), sem("rsum_ready"), sem("prob_ready")
        pT_ps, pT_even, pT_odd = sem("pT_ps"), sem("pT_even"), sem("pT_odd")
        z_ps, z_ready = sem("z_ps"), sem("z_ready")
        o_ps, o_added = sem("o_ps"), sem("o_added")

        block = ctx.enter_context(nc.Block())

        ABANK = [SC[1][0], SC[1][1], PT[0], PT[1]]

        def heads4(t, q):
            return t[:, 8 * (q // 2):8 * (q // 2) + 8, :].rearrange("p (k two) d -> p k two d", two=2)[:, :, q % 2, :]

        def four(bank):
            return bank[:].rearrange("p (k d) -> p k d", k=4)

        def bc(ap, n):
            return ap.unsqueeze(2).to_broadcast([P, ap.shape[1], n])


        N_VAR = 7

        def dve_var(dve, stats, chain_sem, mean, diff, m2, vare, var, base):
            k = base
            nc.vector.tensor_tensor(mean, stats[:, :, 1], stats[:, :, 4], ALU.add).then_inc(chain_sem, 1)
            nc.vector.tensor_tensor(diff, stats[:, :, 1], stats[:, :, 4], ALU.subtract).then_inc(chain_sem, 1)
            nc.vector.tensor_tensor(m2, stats[:, :, 2], stats[:, :, 5], ALU.add).then_inc(chain_sem, 1)
            dve.wait_ge(chain_sem, k + 2)
            nc.vector.scalar_tensor_tensor(diff, diff, 0.25, diff, ALU.mult, ALU.mult).then_inc(chain_sem, 1)
            nc.vector.tensor_scalar(mean, mean, 0.5, None, ALU.mult).then_inc(chain_sem, 1)
            dve.wait_ge(chain_sem, k + 4)
            nc.vector.scalar_tensor_tensor(var, m2, 1.0 / D, diff, ALU.mult, ALU.add).then_inc(chain_sem, 1)
            dve.wait_ge(chain_sem, k + 6)
            nc.vector.tensor_scalar(vare, var, EPS, None, ALU.add).then_inc(chain_sem, 1)

        def is_first(i, n=1):
            return isinstance(i, int) and i < n

        def route_stats(dve, f, i, xs):
            r, s, n = rt[f], R[f], rt[f].n
            for j in range(n):
                ins = nc.vector.bn_stats(r("st", i)[:, j, :], xs[:, j, :])
            ins.then_inc(s["first"], 1)
            dve.wait_ge(s["first"], i + 1)
            b, vars_ = i * (N_VAR + 2), r("vars", i)
            dve_var(dve, r("st", i), s["stats"], r("mean", i)[:], r("diff", i)[:], r("m2", i)[:], vars_[:, 0:n],
                    r("var", i)[:], b)
            dve.wait_ge(s["stats"], b + N_VAR)
            nc.vector.reciprocal(r("rvar", i)[:], vars_[:, 0:n]).then_inc(s["stats"], 1)
            dve.wait_ge(s["stats"], b + N_VAR + 1)
            nc.vector.tensor_tensor(r("ratio", i)[:], r("rvar", i)[:], r("var", i)[:], ALU.mult) \
                .then_inc(s["stats"], 1)
            dve.wait_ge(s["stats"], b + N_VAR + 2)
            nc.vector.tensor_scalar(vars_[:, n:2 * n], r("ratio", i)[:], EPS, None, ALU.add) \
                .then_inc(s["var_ready"], 1)

        def route_rstd(pool, f, i):
            r, s = rt[f], R[f]
            pool.wait_ge(s["var_ready"], i + 1)
            nc.gpsimd.tensor_tensor(r("rstd", i)[:], r("vars", i)[:], mhalf[:, 0:2 * r.n], ALU.pow) \
                .then_inc(s["rstd_ready"], 1)

        def route_norm(dve, f, i, xs, ids):
            r, s, n = rt[f], R[f], rt[f].n
            row = r("row", i)
            mean, rst = r("mean", i), r("rst", i)
            rs, rs2 = r("rstd", i)[:, 0:n], r("rstd", i)[:, n:2 * n]
            amul, cadd = r("amul", i), r("cadd", i)
            dve.wait_ge(s["rstd_ready"], i + 1)
            nc.vector.tensor_tensor(rst[:], rs, rs2, ALU.mult).then_inc(s["norm"], 1)
            nc.vector.tensor_scalar(amul[:], rs, 0.5, 1.0, ALU.mult, ALU.add).then_inc(s["aff"], 1)
            nc.vector.scalar_tensor_tensor(cadd[:], rs, -0.5, mean[:], ALU.mult, ALU.mult).then_inc(s["aff"], 1)
            dve.wait_ge(s["norm"], i + 1)
            if r.ring == 1 and not is_first(i):
                dve.wait_ge(s["scattered"], i * n * 16)
                dve.wait_ge(s["stored"], i * 16)
            for j in range(n):
                ins = nc.vector.tensor_scalar(row[:, j, 0:D], xs[:, j, :], mean[:, j:j + 1], rst[:, j:j + 1],
                                              ALU.subtract, ALU.mult)
            ins.then_inc(s["tok_done"], 1)
            nc.vector.tensor_copy(row[:, :, ROW_ID], ids).then_inc(s["id_set"], 1)
            if f == 0:
                return
            dve.wait_ge(s["aff"], 2 * i + 2)
            for j in range(n):
                ins = nc.vector.tensor_scalar(row[:, j, ROW_RES:ROW_RES + D], xs[:, j, :], amul[:, j:j + 1],
                                              cadd[:, j:j + 1], ALU.mult, ALU.add)
            ins.then_inc(s["x_done"], 1)

        def read_logits(dve, f, i, logits):
            dve.wait_ge(R[f]["logit_ps"], i + 1)
            nc.vector.tensor_copy(rt[f]("lg", i)[:], logits).then_inc(R[f]["logit_read"], 1)

        def route_pick(dve, f, i):
            r, s, n = rt[f], R[f], rt[f].n
            b = i * 4
            lg, cand, hotf = r("lg", i)[:], r("cand", i)[:], r("hotf", i)[:]
            dve.wait_ge(s["logit_read"], i + 1)
            nc.vector.tensor_reduce(r("lmax", i)[:], lg, AX.X, ALU.max).then_inc(s["hots"], 1)
            dve.wait_ge(s["hots"], b + 1)
            nc.vector.tensor_tensor(r("dlt", i)[:], lg, bc(r("lmax", i)[:], NE), ALU.subtract) \
                .then_inc(s["delta_ready"], 1)
            dve.wait_ge(s["delta_ready"], i + 1)
            nc.vector.scalar_tensor_tensor(cand, r("dlt", i)[:], 0.0, rev[:].unsqueeze(1).to_broadcast([P, n, NE]),
                                           ALU.is_ge, ALU.mult).then_inc(s["hots"], 1)
            dve.wait_ge(s["hots"], b + 2)
            nc.vector.tensor_reduce(r("cmax", i)[:], cand, AX.X, ALU.max).then_inc(s["hots"], 1)
            dve.wait_ge(s["hots"], b + 3)
            nc.vector.tensor_tensor(hotf, cand, bc(r("cmax", i)[:], NE), ALU.is_equal).then_inc(s["hots"], 1)
            dve.wait_ge(s["hots"], b + 4)
            nc.vector.tensor_copy(r("hot", i)[:], hotf).then_inc(s["hot_ready"], 1)

        N_FINAL = 11

        def read_ranks(dve, f, i, ranks):
            r, n = rt[f], rt[f].n
            dve.wait_ge(R[f]["rank_ps"], i + 1)
            nc.vector.tensor_copy(r("rkp", i)[:], ranks[:, 0:n, :])
            nc.vector.tensor_copy(r("tot", i)[:], ranks[:, n, :]).then_inc(R[f]["rank_read"], 1)

        def route_final(dve, f, i):
            r, s, n = rt[f], R[f], rt[f].n
            b = i * N_FINAL
            fin, hotf, row = s["final"], r("hotf", i)[:], r("row", i)
            tt, ts, stt = nc.vector.tensor_tensor, nc.vector.tensor_scalar, nc.vector.scalar_tensor_tensor
            tt(r("bsel", i)[:], hotf, ebase[:].unsqueeze(1).to_broadcast([P, n, NE]), ALU.mult).then_inc(fin, 1)
            dve.wait_ge(s["exl_ready"], i + 1)
            nc.vector.tensor_reduce(r("den", i)[:], r("exl", i)[:], AX.X, ALU.add).then_inc(fin, 1)
            if is_first(i):
                dve.wait_ge(consts, 4)
            else:
                dve.wait_ge(s["seen_done"], i)
            dve.wait_ge(s["rank_read"], i + 1)
            tt(r("rk", i)[:], r("rkp", i)[:], r.seen[:].unsqueeze(1).to_broadcast([P, n, NE]), ALU.add).then_inc(fin, 1)
            dve.wait_ge(fin, b + 3)
            tt(r.seen[:], r("tot", i)[:], r.seen[:], ALU.add).then_inc(s["seen_done"], 1)
            tt(r("rsel", i)[:], r("rk", i)[:], hotf, ALU.mult).then_inc(fin, 1)
            nc.vector.tensor_reduce(r("base", i)[:], r("bsel", i)[:], AX.X, ALU.add).then_inc(fin, 1)
            nc.vector.reciprocal(r("rden", i)[:], r("den", i)[:]).then_inc(fin, 1)
            dve.wait_ge(fin, b + 4)
            nc.vector.tensor_reduce(r("rank", i)[:], r("rsel", i)[:], AX.X, ALU.add).then_inc(fin, 1)
            dve.wait_ge(fin, b + 7)
            ts(r("keep", i)[:], r("rank", i)[:], float(CAP), None, ALU.is_lt).then_inc(fin, 1)
            tt(r("d1", i)[:], r("rank", i)[:], r("base", i)[:], ALU.add).then_inc(fin, 1)
            dve.wait_ge(fin, b + 9)
            tt(r("d2", i)[:], r("d1", i)[:], noslot[:, 0:n], ALU.subtract).then_inc(fin, 1)
            stt(row[:, :, ROW_WT], r("keep", i)[:], 0.5, r("rden", i)[:], ALU.mult, ALU.mult).then_inc(s["id_set"], 1)
            dve.wait_ge(fin, b + 10)
            tt(r("d3", i)[:], r("d2", i)[:], r("keep", i)[:], ALU.mult).then_inc(fin, 1)
            dve.wait_ge(s["id_set"], 2 * i + 2)
            dve.wait_ge(fin, b + 11)
            tt(r("dest", i)[:], r("d3", i)[:], noslot[:, 0:n], ALU.add).then_inc(s["dest_ready"], 1)

        def route_scatter(pool, f, i):
            r, s = rt[f], R[f]
            for j in range(r.n):
                nc.gpsimd.indirect_dma_start(
                    out=disp[f][:, :], out_offset=bass.IndirectOffsetOnAxis(r("dest", i)[:, j:j + 1], 0),
                    in_=r("row", i)[:, j, :], in_offset=None, bounds_check=SLOTS - 1,
                    oob_is_err=False).then_inc(s["scattered"], 16)

        def pe_ranks(f, i, ps):
            r, n = rt[f], rt[f].n
            hot = r("hot", i)
            for j in range(n + 1):
                earlier = list(range(min(j, n)))
                if j < n:
                    ins = nc.tensor.matmul(ps[:, j, :], before[:], hot[:, j, :], start=True, stop=not earlier)
                for k in earlier:
                    ins = nc.tensor.matmul(ps[:, j, :], ones[:], hot[:, k, :], start=j == n and k == 0,
                                           stop=k == earlier[-1])
            return ins

        UPS = [[SC[1][0], SC[1][1]], [PT[0], PT[1]]]
        DNS = [PJ, Z]

        def sp_rows(sp, E):
            if E >= 4:
                sp.wait_ge(eres_ready, E - 3)
            e = E % NE
            sp.dma_start(ein[E % 4][:], disp[E // NE][e * CAP:(e + 1) * CAP, :].rearrange("(c p) d -> p c d", p=P)) \
                .then_inc(ein_in[E % 4], 16)

        def pe_expert_in(pe, E):
            pe.wait_ge(ein_in[E % 4], 16 * (E // 4 + 1))
            if E >= 2:
                pe.wait_ge(ein_read, E - 1)
            for c in range(2):
                ins = nc.tensor.transpose(SC[0][E % 2][:, c * P:(c + 1) * P], ein[E % 4][:, c, 0:D], ident[:])
            ins.then_inc(ein_ps, 1)

        def pe_expert_up(pe, E):
            if E < NE:
                pe.wait_ge(ewi_split, E + 1)
                pe.wait_ge(ew_in[E], 32)
            pe.wait_ge(ein_ready, E + 1)
            if E >= 2:
                pe.wait_ge(gelu_done, 2 * E - 2)
            for i in range(NI):
                o = UPS[E % 2][i // 2][:, (i % 2) * CAP:(i % 2 + 1) * CAP]
                hi, lo = ewi_hi[E % NE][:, i * P:(i + 1) * P], ewi_lo[E % NE][:, i * P:(i + 1) * P]
                nc.tensor.matmul(o, hi, eTh[E % 2][:], start=True, stop=False)
                nc.tensor.matmul(o, lo, eTh[E % 2][:], start=False, stop=False)
                ins = nc.tensor.matmul(o, hi, eTl[E % 2][:], start=False, stop=True)
                if i % 2:
                    ins.then_inc(up_ps, 1)

        def pe_expert_down(pe, E):
            pe.wait_ge(gelu_done, 2 * E + 2)
            if E >= 2:
                pe.wait_ge(eres_ready, E - 1)
            for c in range(2):
                for i in range(NI):
                    ins = nc.tensor.matmul(DNS[E % 2][:, c * D:(c + 1) * D], ehT[E % 2][:, i, c * P:(c + 1) * P],
                                           ewo[E % NE][:, i, :], start=i == 0, stop=i == NI - 1)
            ins.then_inc(down_ps, 1)

        def act_expert(act, E):
            for u in range(2):
                act.wait_ge(up_ps, 2 * E + u + 1)
                if u == 0 and E >= 2:
                    act.wait_ge(down_ps, E - 1)
                nc.scalar.activation(ehT[E % 2][:, 2 * u:2 * u + 2, :].rearrange("p i c -> p (i c)"),
                                     UPS[E % 2][u][:], ACT.Gelu).then_inc(gelu_done, 1)

        def dve_expert_in(dve, E):
            dve.wait_ge(ein_ps, E + 1)
            if E >= 1:
                dve.wait_ge(ein_ready, E)
            nc.vector.tensor_scalar(einT[:], SC[0][E % 2][:, 0:CAP], gcol[:], bcol[:],
                                    ALU.mult, ALU.add).then_inc(ein_read, 1)
            if E >= 2:
                dve.wait_ge(up_ps, 2 * E - 2)
            dve.wait_ge(ein_read, E + 1)
            nc.vector.tensor_copy(eTh[E % 2][:], einT[:]).then_inc(ein_hi, 1)
            dve.wait_ge(ein_hi, E + 1)
            nc.vector.tensor_tensor(eTl[E % 2][:], einT[:], eTh[E % 2][:].bitcast(F32), ALU.subtract) \
                .then_inc(ein_ready, 1)

        def dve_expert_out(dve, E):
            rows, par = ein[E % 4], E % 2
            if E >= 2:
                dve.wait_ge(eres_out[par], 32 * (E // 2))
            nc.vector.tensor_copy(eid[par][:], rows[:, :, ROW_ID]).then_inc(eid_ready, 1)
            dve.wait_ge(down_ps, E + 1)
            for c in range(2):
                ins = nc.vector.scalar_tensor_tensor(
                    eres[par][:, c, :], DNS[par][:, c * D:(c + 1) * D], rows[:, c, ROW_WT:ROW_WT + 1],
                    rows[:, c, ROW_RES:ROW_RES + D], ALU.mult, ALU.add)
            ins.then_inc(eres_ready, 1)

        def pool_expert_out(pool, E, target):
            pool.wait_ge(eid_ready, E + 1)
            pool.wait_ge(eres_ready, E + 1)
            for c in range(2):
                nc.gpsimd.indirect_dma_start(
                    out=target, out_offset=bass.IndirectOffsetOnAxis(eid[E % 2][:, c:c + 1], 0),
                    in_=eres[E % 2][:, c, :], in_offset=None, bounds_check=NT * P - 1,
                    oob_is_err=False).then_inc(eres_out[E % 2], 16)

        def experts(f, take_in, up, down):
            E0 = NE * f
            take_in(E0)
            take_in(E0 + 1)
            up(E0)
            for E in range(E0, E0 + NE):
                if E + 2 < E0 + NE:
                    take_in(E + 2)
                if E + 1 < E0 + NE:
                    up(E + 1)
                down(E)

        def sp_experts(sp, f):
            sp.wait_ge(R[f]["scattered"], NT * 16)
            for E in range(NE * f, NE * f + NE):
                sp_rows(sp, E)

        x1t = x1_dram.rearrange("(t p) d -> p t d", p=P)
        xt = x.rearrange("b (t p) d -> p (b t) d", p=P)
        ot = out.rearrange("b (t p) d -> p (b t) d", p=P)

        NV = 4 * BT
        VPS = Z[:, SEQ:2 * SEQ]
        HALF = PJ[:, 0:SEQ]
        MIDDLE = {2: ("rank", -2), 3: ("o", -1), 4: ("yT", 1), 6: ("tT", -1), 7: ("logit", -1)}
        PJ_READ = {"g": (g_lo, NPAIR), "rank": (R[1]["rank_read"], 1), "o": (o_added, 1), "yT": (yT_lo, 1),
                   "tT": (R[1]["tT_ready"], 1), "logit": (R[1]["logit_read"], 1)}

        def valid(b):
            return not isinstance(b, int) or 0 <= b < NB

        def at(b, p):
            return b * NPAIR + p

        def run(eng, batch):
            batch(0, 0)
            batch(1, 1)
            with eng.Fori(1, NB // 2 - 1) as k:
                batch(2 * k, 0)
                batch(2 * k + 1, 1)
            batch(NB - 2, 0)
            batch(NB - 1, 1)
            batch(NB, 0)
            batch(NB + 1, 1)

        def seq(b):
            return slice(BT * b, BT * b + BT) if isinstance(b, int) else bass.ds(BT * b, BT)

        def back(b, p, k):
            return (b, p - k) if p >= k else (b - 1, p - k + NPAIR)

        def fwd(b, p):
            return (b, p + 1) if p + 1 < NPAIR else (b + 1, 0)

        @block.sync
        def _(sp):
            for g in range(NG):
                sp.dma_start(X[:, g * GT:(g + 1) * GT, :], xt[:, g * GT:(g + 1) * GT, :]).then_inc(x_in[g], 16)

            def empty_slots(f):
                for q in range(SLOTS // P // 4):
                    sp.dma_start(disp[f][q * 4 * P:(q + 1) * 4 * P, :].rearrange("(r p) d -> p r d", p=P),
                                 empty[:]).then_inc(disp_emptied[f], 16)
            sp.wait_ge(empty_in_done, 16)
            empty_slots(0)
            sp.dma_start(wqT[:], w_qT.rearrange("(a p) d -> p a d", p=P)).then_inc(watt_in, 16)
            sp.dma_start(wkT[:], w_kT.rearrange("(a p) d -> p a d", p=P)).then_inc(watt_in, 16)
            sp.dma_start(wv[:], w_v).then_inc(watt_in, 16)
            sp.dma_start(wos[:], w_o.rearrange("(a p) d -> p a d", p=P)).then_inc(watt_in, 16)
            for e in range(NE):
                sp.dma_start(ewo[e][:], wo[e].rearrange("(i p) d -> p i d", p=P)).then_inc(ew_in[e], 16)
            for g in range(NG):
                sp.wait_ge(R[0]["x_done"], g + 1)
                sp.dma_start(x1t[:, g * GT:(g + 1) * GT, :], rt[0]("row", g)[:, :, ROW_RES:ROW_RES + D]) \
                    .then_inc(R[0]["stored"], 16)
            sp.wait_ge(R[0]["tok_done"], NG)
            for e in range(NE):
                sp.dma_start(ewi[e], wi[e]).then_inc(ew_in[e], 16)
            sp_experts(sp, 0)
            empty_slots(1)
            for par in range(2):
                sp.wait_ge(eres_out[par], 16 * NE)

            def load_x1(b, par):
                if not is_first(b, 2):
                    sp.wait_ge(x_plus_ya, b - 1)
                sp.dma_start(x1[par][:], x1t[:, seq(b), :]).then_inc(x1_in[par], 16)

            def batch(b, par):
                if valid(b + 2):
                    load_x1(b + 2, par)
                if valid(b - 1):
                    sp.wait_ge(R[1]["x_done"], b)
                    sp.dma_start(ot[:, seq(b - 1), :], rt[1]("row", 0)[:, :, ROW_RES:ROW_RES + D]) \
                        .then_inc(R[1]["stored"], 16)
            load_x1(0, 0)
            load_x1(1, 1)
            run(sp, batch)
            sp_experts(sp, 1)
            for par in range(2):
                sp.wait_ge(eres_out[par], 32 * NE)
            sp.wait_ge(R[1]["stored"], 16 * NB)

        @block.gpsimd
        def _(pool):
            nc.gpsimd.memset(mhalf[:], -0.5).then_inc(consts, 1)
            nc.gpsimd.memset(ones[:], 1.0).then_inc(consts, 1)
            nc.gpsimd.memset(rt[0].seen[:], 0.0).then_inc(consts, 1)
            nc.gpsimd.memset(rt[1].seen[:], 0.0).then_inc(consts, 1)
            pool.wait_ge(consts, 4)

            def scatter(g):
                pool.wait_ge(R[0]["x_done"], g + 1)
                pool.wait_ge(R[0]["dest_ready"], g + 1)
                route_scatter(pool, 0, g)
            for g in range(NG):
                route_rstd(pool, 0, g)
            pool.wait_ge(disp_emptied[0], 16 * (SLOTS // P // 4))
            for g in range(NG):
                scatter(g)
            pool.wait_ge(wv_hi, 1)
            nc.gpsimd.tensor_tensor(wvl[:], wv[:], wvh[:].bitcast(F32), ALU.subtract).then_inc(wv_lo, 1)
            pool.wait_ge(R[0]["stored"], 16 * NG)
            for e in range(NE):
                pool_expert_out(pool, e, x1_dram[:, :])
            pool.wait_ge(disp_emptied[1], 16 * (SLOTS // P // 4))

            def prep_rstd(b):
                pool.wait_ge(c_chain, N_VAR * (b + 1))
                nc.gpsimd.tensor_tensor(c_rs[:], c_vare[:], mhalf[:, 0:BT], ALU.pow).then_inc(c_rstd, 1)

            def batch(b, par):
                for p in range(NPAIR):
                    pb, pp = back(b, p, 1)
                    if p == 3 and valid(b - 2):
                        pool.wait_ge(R[1]["dest_ready"], b - 1)
                    if valid(pb):
                        pool.wait_ge(rsum_ready, at(pb, pp) + 1)
                        q = pp % 4
                        v = prob[q][:].rearrange("p c h k -> p (c h) k")
                        nc.gpsimd.tensor_tensor(v, v, bc(rsum[q][:], SEQ), ALU.mult).then_inc(prob_ready, 1)
                    if p == 1 and valid(b + 1):
                        prep_rstd(b + 1)
                    if p == 3 and valid(b - 2):
                        route_scatter(pool, 1, 0)
                    if p == 4 and valid(b - 1):
                        route_rstd(pool, 1, b - 1)
            prep_rstd(0)
            run(pool, batch)
            pool.wait_ge(R[1]["stored"], 16 * NB)
            for e in range(NE):
                pool_expert_out(pool, NE + e, out.rearrange("b s d -> (b s) d"))

        @block.scalar
        def _(act):
            for tile, source in ((ident, ident_in), (tri_f, before_in), (tokid, tokid_in), (gcol, gamma), (bcol, beta),
                                 (gateT, gate), (rev, rev_in), (ebase, ebase_in), (noslot, noslot_in)):
                act.dma_start(tile[:], source).then_inc(const_in, 16)
            act.dma_start(empty[:], empty_in).then_inc(empty_in_done, 16)
            act.wait_ge(consts, 4)
            act.wait_ge(const_in, 144)

            def route_tT(f, i, banks, width):
                r, s = rt[f], R[f]
                for k, bank in enumerate(banks):
                    act.wait_ge(s["tT_ps"], len(banks) * i + k + 1)
                    nc.scalar.activation(r("tokT", i)[:].rearrange("p n q -> p (n q)")[:, k * width:(k + 1) * width],
                                         bank[:, 0:width], ACT.Identity, bias=bcol[:], scale=gcol[:]) \
                        .then_inc(s["tT_ready"], 1)

            def route_exp(f, i):
                r, s = rt[f], R[f]
                act.wait_ge(s["delta_ready"], i + 1)
                nc.scalar.activation(r("exl", i)[:], r("dlt", i)[:], ACT.Exp).then_inc(s["exl_ready"], 1)

            def residual(g):
                amul, cadd, row = rt[0]("amul", g), rt[0]("cadd", g), rt[0]("row", g)
                act.wait_ge(R[0]["aff"], 2 * g + 2)
                for j in range(GT):
                    ins = nc.scalar.activation(row[:, j, ROW_RES:ROW_RES + D], X[:, g * GT + j, :], ACT.Identity,
                                               bias=cadd[:, j:j + 1], scale=amul[:, j:j + 1])
                ins.then_inc(R[0]["x_done"], 1)
            for g in range(NG):
                route_tT(0, g, [SC[0][0], SC[0][1]], 512)
                if g:
                    route_exp(0, g - 1)
                residual(g)
            route_exp(0, NG - 1)
            act.wait_ge(watt_in, 64)
            nc.scalar.activation(wvh[:], wv[:], ACT.Copy).then_inc(wv_hi, 1)
            for q in range(4):
                act.wait_ge(a_ps, q + 1)
                nc.scalar.activation(heads4(ah, q), four(ABANK[q]), ACT.Copy).then_inc(a_hi, 1)
            for e in range(NE):
                act.wait_ge(ew_in[e], 32)
                nc.scalar.activation(ewi_hi[e][:], ewi[e], ACT.Copy).then_inc(ewi_rounded, 1)
            for E in range(NE):
                act_expert(act, E)

            def prep_hi(b, par):
                act.wait_ge(yT_ps, b + 1)
                nc.scalar.activation(yTh[par][:], HALF, ACT.Copy).then_inc(yT_hi, 1)

            def g_hi_part(b, p):
                act.wait_ge(g_ps, at(b, p) + 1)
                if not (isinstance(b, int) and at(b, p) < 2):
                    act.wait_ge(scores_ps, 2 * at(b, p) - 2)
                nc.scalar.activation(Gh[p % 2][:], PJ[:], ACT.Copy).then_inc(g_hi, 1)

            def exps(p, c):
                for h in range(2):
                    k = 2 * c + h
                    ins = nc.scalar.activation(
                        prob[p % 4][:, c, h, :], SC[p % 2][c][:, h * SEQ:(h + 1) * SEQ], ACT.Exp,
                        bias=nbias[p % 4][:, k:k + 1], scale=SCALE, accum_out=sums[p % 4][:, k:k + 1])
                ins.then_inc(exp_done, 1)

            def batch(b, par):
                for p in range(NPAIR):
                    zb, zp = back(b, p, 4)
                    if valid(zb):
                        act.wait_ge(z_ps, at(zb, zp) + 1)
                        zpar = par if p >= 4 else 1 - par
                        if not is_first(zb, 2):
                            act.wait_ge(o_ps, zb - 1)
                        nc.scalar.activation(zT[zpar][:, zp, :], Z[:, 0:SEQ], ACT.Copy).then_inc(z_ready, 1)
                    nb, np_ = fwd(b, p)
                    if valid(nb):
                        g_hi_part(nb, np_)
                    pb, pp = back(b, p, 1)
                    if valid(pb):
                        act.wait_ge(bias_ready, at(pb, pp) + 1)
                        if not (isinstance(pb, int) and at(pb, pp) < 4):
                            act.wait_ge(pT_ps, 2 * at(pb, pp) - 6)
                        exps(pp, 0)
                    if valid(b):
                        act.wait_ge(v_ps, NV * b + p + 1)
                        nc.scalar.activation(V[:, p % BT, (p // BT) * SEQ:(p // BT + 1) * SEQ], VPS,
                                             ACT.Copy).then_inc(v_ready, 1)
                    if valid(pb):
                        exps(pp, 1)
                    if p == 4 and valid(b + 1):
                        prep_hi(b + 1, 1 - par)
                    if p == 6 and valid(b - 1):
                        route_tT(1, b - 1, [HALF], SEQ)
                    tb, tp = back(b, p, 2)
                    if valid(tb):
                        act.wait_ge(pT_ps, 2 * at(tb, tp) + 1)
                        if not (isinstance(tb, int) and at(tb, tp) < 2):
                            act.wait_ge(z_ps, at(tb, tp) - 1)
                        nc.scalar.activation(probT[tp % 2][0].rearrange("p j q -> p (j q)"), PT[0][:],
                                             ACT.Copy).then_inc(pT_even, 1)
                    if p == 0 and valid(b - 2):
                        route_exp(1, b - 2)
            prep_hi(0, 0)
            g_hi_part(0, 0)
            run(act, batch)
            for E in range(NE, 2 * NE):
                act_expert(act, E)

        @block.vector
        def _(dve):

            logits8 = PJ[:, 0:GT * NE].rearrange("p (n e) -> p n e", e=NE)
            ranks8 = Z[:, 0:(GT + 1) * NE].rearrange("p (n e) -> p n e", e=NE)

            def stats(g):
                dve.wait_ge(x_in[g], 16)
                route_stats(dve, 0, g, X[:, g * GT:(g + 1) * GT, :])

            def norm(g):
                route_norm(dve, 0, g, X[:, g * GT:(g + 1) * GT, :], tokid[:, g * GT:(g + 1) * GT])

            def pick(g):
                read_logits(dve, 0, g, logits8)
                route_pick(dve, 0, g)

            def final(g):
                read_ranks(dve, 0, g, ranks8)
                route_final(dve, 0, g)
            stats(0)
            stats(1)
            dve.wait_ge(const_in, 144)
            nc.vector.tensor_copy(before[:], tri_f[:]).then_inc(before_ready, 1)
            for stage, g in ((norm, 0), (stats, 2), (norm, 1), (stats, 3), (pick, 0), (final, 0), (norm, 2), (pick, 1),
                             (norm, 3), (final, 1), (pick, 2), (final, 2), (pick, 3), (final, 3)):
                stage(g)
            for q in range(4):
                dve.wait_ge(a_hi, q + 1)
                nc.vector.tensor_tensor(heads4(al, q), four(ABANK[q]), heads4(ah, q).bitcast(F32),
                                        ALU.subtract).then_inc(a_lo, 1)
            for e in range(NE):
                dve.wait_ge(ewi_rounded, e + 1)
                nc.vector.tensor_tensor(ewi_lo[e][:], ewi[e], ewi_hi[e][:].bitcast(F32), ALU.subtract) \
                    .then_inc(ewi_split, 1)
            experts(0, lambda E: dve_expert_in(dve, E), lambda E: None, lambda E: dve_expert_out(dve, E))

            def prep_stats(b, par):
                dve.wait_ge(x1_in[par], 8 * (b - par) + 16)
                for j in range(BT):
                    ins = nc.vector.bn_stats(c_st[:, j, :], x1[par][:, j, :])
                ins.then_inc(c_stats, 1)
                dve.wait_ge(c_stats, b + 1)
                dve_var(dve, c_st, c_chain, c_mean[:], c_diff[:], c_m2[:], c_vare[:], c_var_[:],
                        b * N_VAR)

            def prep_norm(b, par):
                dve.wait_ge(c_rstd, b + 1)
                nc.vector.tensor_scalar(c_mul[:], c_rs[:], 1.0, None, ALU.add).then_inc(c_aff, 1)
                nc.vector.scalar_tensor_tensor(c_add[:], c_rs[:], -1.0, c_mean[:], ALU.mult, ALU.mult) \
                    .then_inc(c_aff, 1)
                if not is_first(b):
                    dve.wait_ge(yT_ps, b)
                for j in range(BT):
                    ins = nc.vector.tensor_scalar(ya[:, j, :], x1[par][:, j, :], c_mean[:, j:j + 1],
                                                  c_rs[:, j:j + 1], ALU.subtract, ALU.mult)
                ins.then_inc(ya_ready, 1)

            def prep_x1y(b, par):
                dve.wait_ge(c_aff, 2 * b + 2)
                for j in range(BT):
                    ins = nc.vector.tensor_scalar(x1y[par][:, j, :], x1[par][:, j, :], c_mul[:, j:j + 1],
                                                  c_add[:, j:j + 1], ALU.mult, ALU.add)
                ins.then_inc(x_plus_ya, 1)

            def prep_lo(b, par):
                dve.wait_ge(yT_hi, b + 1)
                nc.vector.tensor_tensor(yTl[par][:], HALF, yTh[par][:].bitcast(F32),
                                        ALU.subtract).then_inc(yT_lo, 1)

            def g_lo_part(b, p):
                dve.wait_ge(g_hi, at(b, p) + 1)
                nc.vector.tensor_tensor(Gl[p % 2][:], PJ[:], Gh[p % 2][:].bitcast(F32), ALU.subtract) \
                    .then_inc(g_lo, 1)

            def batch(b, par):
                for p in range(NPAIR):
                    nb, np_ = fwd(b, p)
                    if valid(nb):
                        g_lo_part(nb, np_)
                    if valid(b):
                        g = at(b, p)
                        for c in range(2):
                            dve.wait_ge(scores_ps, 2 * g + c + 1)
                            ins = nc.vector.tensor_reduce(
                                mx[p % 4][:, 2 * c:2 * c + 2],
                                SC[p % 2][c][:].rearrange("p (h k) -> p h k", h=2), AX.X, ALU.max)
                        ins.then_inc(max_done, 1)
                        dve.wait_ge(max_done, g + 1)
                        nc.vector.tensor_scalar(nbias[p % 4][:], mx[p % 4][:], -SCALE, None,
                                                ALU.mult).then_inc(bias_ready, 1)
                    pb, pp = back(b, p, 1)
                    if valid(pb):
                        dve.wait_ge(exp_done, 2 * at(pb, pp) + 2)
                        if not (isinstance(pb, int) and at(pb, pp) < 4):
                            dve.wait_ge(prob_ready, at(pb, pp) - 3)
                        nc.vector.reciprocal(rsum[pp % 4][:], sums[pp % 4][:]).then_inc(rsum_ready, 1)
                    if p == 3 and valid(b - 2):
                        route_final(dve, 1, b - 2)
                    if p == 3 and valid(b + 1):
                        prep_norm(b + 1, 1 - par)
                    if p == 2 and valid(b - 2):
                        read_ranks(dve, 1, b - 2, PJ[:, 0:(BT + 1) * NE].rearrange("p (n e) -> p n e", e=NE))
                    if p == 3 and valid(b - 1):
                        dve.wait_ge(o_ps, b)
                        nc.vector.tensor_tensor(x2[:], HALF.rearrange("p (t d) -> p t d", d=D),
                                                x1y[1 - par][:], ALU.add).then_inc(o_added, 1)
                    if p == 4 and valid(b + 1):
                        prep_lo(b + 1, 1 - par)
                    if p == 7 and valid(b - 1):
                        read_logits(dve, 1, b - 1, PJ[:, 0:BT * NE].rearrange("p (n e) -> p n e", e=NE))
                    tb, tp = back(b, p, 2)
                    if valid(tb):
                        dve.wait_ge(pT_ps, 2 * at(tb, tp) + 2)
                        if not (isinstance(tb, int) and at(tb, tp) < 2):
                            dve.wait_ge(z_ps, at(tb, tp) - 1)
                        nc.vector.tensor_copy(probT[tp % 2][1].rearrange("p j q -> p (j q)"),
                                              PT[1][:]).then_inc(pT_odd, 1)
                    if p == 0 and valid(b + 1):
                        prep_stats(b + 1, 1 - par)
                    if p == 3 and valid(b - 1):
                        dve.wait_ge(o_added, b)
                        route_stats(dve, 1, b - 1, x2)
                    if p == 4 and valid(b + 1):
                        prep_x1y(b + 1, 1 - par)
                    if p == 5 and valid(b - 1):
                        route_norm(dve, 1, b - 1, x2, tokid[:, seq(b - 1)])
                    if p == 7 and valid(b - 1):
                        route_pick(dve, 1, b - 1)
            prep_stats(0, 0)
            prep_norm(0, 0)
            prep_x1y(0, 0)
            prep_lo(0, 0)
            g_lo_part(0, 0)
            run(dve, batch)
            experts(1, lambda E: dve_expert_in(dve, E), lambda E: None, lambda E: dve_expert_out(dve, E))


        @block.tensor
        def _(pe):
            pe.wait_ge(const_in, 144)
            pe.wait_ge(consts, 4)
            pe.wait_ge(before_ready, 1)
            r, s = rt[0], R[0]

            def transposes(g):
                pe.wait_ge(s["tok_done"], g + 1)
                if g:
                    pe.wait_ge(s["tT_ready"], 2 * g)
                for j in range(GT):
                    ins = nc.tensor.transpose(SC[0][j // 4][:, (j % 4) * P:(j % 4 + 1) * P],
                                              r("row", g)[:, j, 0:D], ident[:])
                    if j % 4 == 3:
                        ins.then_inc(s["tT_ps"], 1)

            def logits(g):
                if g:
                    pe.wait_ge(s["logit_read"], g)
                for j in range(GT):
                    if j % 4 == 0:
                        pe.wait_ge(s["tT_ready"], 2 * g + j // 4 + 1)
                    ins = nc.tensor.matmul(PJ[:, j * NE:(j + 1) * NE], r("tokT", g)[:, j, :], gateT[:],
                                           start=True, stop=True)
                ins.then_inc(s["logit_ps"], 1)

            def ranks(g):
                pe.wait_ge(s["hot_ready"], g + 1)
                if g:
                    pe.wait_ge(s["rank_read"], g)
                pe_ranks(0, g, Z[:, 0:(GT + 1) * NE].rearrange("p (n e) -> p n e", e=NE)).then_inc(s["rank_ps"], 1)
            transposes(0)
            for g in range(NG):
                logits(g)
                if g + 1 < NG:
                    transposes(g + 1)
                ranks(g)
            pe.wait_ge(watt_in, 64)
            for q in range(4):
                for k in range(4):
                    h = 8 * (q // 2) + 2 * k + q % 2
                    half = slice(DK * (h % 2), DK * (h % 2) + DK)
                    ins = nc.tensor.matmul(ABANK[q][:, k * D:(k + 1) * D], wqT[half, h // 2, :],
                                           wkT[half, h // 2, :], start=True, stop=True)
                ins.then_inc(a_ps, 1)
            pe.wait_ge(a_lo, 4)
            pe.wait_ge(R[0]["rank_read"], NG)
            experts(0, lambda E: pe_expert_in(pe, E), lambda E: pe_expert_up(pe, E), lambda E: pe_expert_down(pe, E))
            pe.wait_ge(eres_ready, NE)
            pe.wait_ge(wv_lo, 1)

            last = [None]

            def take(b, kind, u, db):
                if last[0] is not None:
                    k, lu, ldb = last[0]
                    s, per = PJ_READ[k]
                    pe.wait_ge(s, per * (b + ldb) + lu + 1)
                last[0] = (kind, u, db)

            def pe_yT(b, par):
                pe.wait_ge(ya_ready, b + 1)
                for j in range(BT):
                    ins = nc.tensor.transpose(PJ[:, j * P:(j + 1) * P], ya[:, j, :], ident[:])
                ins.then_inc(yT_ps, 1)

            def pe_g(b, p, par):
                if p == 0:
                    pe.wait_ge(yT_lo, b + 1)
                for h in range(2):
                    hh = 2 * p + h
                    o = PJ[:, h * SEQ:(h + 1) * SEQ]
                    nc.tensor.matmul(o, ah[:, hh, :], yTh[par][:], start=True, stop=False)
                    nc.tensor.matmul(o, al[:, hh, :], yTh[par][:], start=False, stop=False)
                    ins = nc.tensor.matmul(o, ah[:, hh, :], yTl[par][:], start=False, stop=True)
                ins.then_inc(g_ps, 1)

            def pe_transpose_probs(b, p, h):
                tb, tp = back(b, p, 2)
                if valid(tb):
                    g = at(tb, tp)
                    if h == 0:
                        pe.wait_ge(prob_ready, g + 1)
                    if not (isinstance(tb, int) and g < 1):
                        pe.wait_ge([pT_even, pT_odd][h], g)
                    for j in range(2):
                        for c in range(2):
                            ins = nc.tensor.transpose(
                                PT[h][:, j * SEQ + c * P:j * SEQ + (c + 1) * P],
                                prob[tp % 4][:, c, h, j * P:(j + 1) * P], ident[:])
                    ins.then_inc(pT_ps, 1)

            def pe_v(b, par, p):
                zb, zp = back(b, p, 4)
                if valid(zb):
                    pe.wait_ge(z_ready, at(zb, zp) + 1)
                elif p:
                    pe.wait_ge(v_ready, p)
                part = slice((p // BT) * SEQ, (p // BT + 1) * SEQ)
                t = slice((p % BT) * P, (p % BT + 1) * P)
                nc.tensor.matmul(VPS, yTh[par][:, t], wvh[:, part], start=True, stop=False)
                nc.tensor.matmul(VPS, yTh[par][:, t], wvl[:, part], start=False, stop=False)
                nc.tensor.matmul(VPS, yTl[par][:, t], wvh[:, part], start=False, stop=True).then_inc(v_ps, 1)

            def middle(b, par, p):
                kind, db = MIDDLE[p]
                tb = b + db
                if not valid(tb):
                    return
                if kind == "yT":
                    take(b, kind, 0, db)
                    pe_yT(tb, 1 - par)
                elif kind == "o":
                    pe.wait_ge(z_ready, at(tb, NPAIR - 1) + 1)
                    take(b, kind, 0, db)
                    for c in range(BT):
                        for k in range(NPAIR):
                            ins = nc.tensor.matmul(PJ[:, c * D:(c + 1) * D], zT[1 - par][:, k, c * P:(c + 1) * P],
                                                   wos[:, k, :], start=k == 0, stop=k == NPAIR - 1)
                    ins.then_inc(o_ps, 1)
                elif kind == "tT":
                    pe.wait_ge(R[1]["tok_done"], tb + 1)
                    take(b, kind, 0, db)
                    for j in range(BT):
                        ins = nc.tensor.transpose(PJ[:, j * P:(j + 1) * P], rt[1]("row", 0)[:, j, 0:D], ident[:])
                    ins.then_inc(R[1]["tT_ps"], 1)
                elif kind == "logit":
                    pe.wait_ge(R[1]["tT_ready"], tb + 1)
                    take(b, kind, 0, db)
                    for j in range(BT):
                        ins = nc.tensor.matmul(PJ[:, j * NE:(j + 1) * NE], rt[1]("tokT", 0)[:, j, :], gateT[:],
                                               start=True, stop=True)
                    ins.then_inc(R[1]["logit_ps"], 1)
                elif kind == "rank":
                    pe.wait_ge(R[1]["hot_ready"], tb + 1)
                    take(b, kind, 0, db)
                    pe_ranks(1, 0, PJ[:, 0:(BT + 1) * NE].rearrange("p (n e) -> p n e", e=NE)) \
                        .then_inc(R[1]["rank_ps"], 1)

            def batch(b, par):
                for p in range(NPAIR):
                    nb, np_ = fwd(b, p)
                    if valid(nb):
                        take(b, "g", np_, 0 if p + 1 < NPAIR else 1)
                        pe_g(nb, np_, par if p + 1 < NPAIR else 1 - par)
                    if valid(b):
                        g = at(b, p)
                        pe.wait_ge(g_lo, g + 1)
                        if not (isinstance(b, int) and g < 2):
                            pe.wait_ge(exp_done, 2 * g - 2)
                        for c in range(2):
                            if c == 1:
                                pe_v(b, par, p)
                            for h in range(2):
                                o = SC[p % 2][c][:, h * SEQ:(h + 1) * SEQ]
                                q = slice(h * SEQ + c * P, h * SEQ + (c + 1) * P)
                                nc.tensor.matmul(o, Gh[p % 2][:, q], yTh[par][:], start=True, stop=False)
                                nc.tensor.matmul(o, Gh[p % 2][:, q], yTl[par][:], start=False, stop=False)
                                ins = nc.tensor.matmul(o, Gl[p % 2][:, q], yTh[par][:], start=False, stop=True)
                            ins.then_inc(scores_ps, 1)
                    pe_transpose_probs(b, p, 0)
                    if p in MIDDLE:
                        middle(b, par, p)
                    pe_transpose_probs(b, p, 1)
                    zb, zp = back(b, p, 3)
                    if valid(zb):
                        g = at(zb, zp)
                        pe.wait_ge(pT_even, g + 1)
                        pe.wait_ge(pT_odd, g + 1)
                        pe.wait_ge(v_ready, NV * zb + BT * (zp // 2 + 1))
                        if not valid(b) and zp + zb:
                            pe.wait_ge(z_ready, g)
                        if valid(b):
                            pe.wait_ge(v_ready, NV * b + p + 1)
                        for j in range(2):
                            for h in range(2):
                                ins = nc.tensor.matmul(
                                    Z[DK * h:DK * h + DK, 0:SEQ], V[:, j, (2 * zp + h) * DK:(2 * zp + h + 1) * DK],
                                    probT[zp % 2][h][:, j, :], start=j == 0, stop=j == 1)
                        ins.then_inc(z_ps, 1)
                k, u, db = last[0]
                last[0] = (k, u, db - 1)
            take(0, "yT", 0, 0)
            pe_yT(0, 0)
            take(0, "g", 0, 0)
            pe_g(0, 0, 0)
            run(pe, batch)
            pe.wait_ge(R[1]["rank_read"], NB)
            experts(1, lambda E: pe_expert_in(pe, E), lambda E: pe_expert_up(pe, E), lambda E: pe_expert_down(pe, E))


_INS = ["x", "w_qT", "w_kT", "w_v", "w_o", "gate", "gamma", "beta", "wi", "wo", "ident", "before", "ebase", "rev",
        "noslot", "tokid", "empty"]


def kernel(**inputs):
    from concourse import bacc as _bacc
    from concourse.bass_utils import run_bass_kernel_spmd as _run

    a = {k: np.asarray(v) for k, v in inputs.items()}
    p = np.arange(P)
    data = {
        "x": a["L0_attn_x"],
        "w_qT": a["L0_attn_w_q"].transpose(0, 2, 1).reshape(NH * DK, D),
        "w_kT": a["L0_attn_w_k"].transpose(0, 2, 1).reshape(NH * DK, D),
        "w_v": a["L0_attn_w_v"].transpose(1, 0, 2).reshape(D, NH * DK),
        "w_o": a["L0_attn_w_o"],
        "gate": a["L0_ffn_gate_weight"].T,
        "gamma": a["L0_ffn_ln_gamma"].reshape(D, 1),
        "beta": a["L0_ffn_ln_beta"].reshape(D, 1),
        "wi": a["L0_ffn_wi"],
        "wo": a["L0_ffn_wo"],
        "ident": np.eye(P, dtype=np.float32),
        "before": np.triu(np.ones((P, P), np.float32), 1),
        "ebase": np.tile(np.arange(NE, dtype=np.float32) * CAP, (P, 1)),
        "rev": np.tile(np.arange(NE, 0, -1, dtype=np.float32), (P, 1)),
        "noslot": (NOSLOT + np.arange(GT)[None, :] * P + p[:, None]).astype(np.float32),
    }
    data["tokid"] = (np.arange(NT)[None, :] * P + p[:, None]).astype(np.float32)
    data["empty"] = np.zeros((P, 4, ROW), np.float32)
    data["empty"][:, :, ROW_ID] = NOTOK + p[:, None]
    nc = _bacc.Bacc("TRN2", target_bir_lowering=False, num_devices=1)
    arrays, args = {}, []
    for name in _INS:
        v = np.ascontiguousarray(data[name])
        arrays[f"in_{name}_dram"] = v
        args.append(nc.dram_tensor(f"in_{name}_dram", v.shape, mybir.dt.from_np(v.dtype), kind="ExternalInput").ap())
    out = nc.dram_tensor("out_0_dram", (NB, SEQ, D), F32, kind="ExternalOutput").ap()
    macaron_kernel(nc, *args, out)
    r = _run(nc, [arrays], core_ids=[0])
    return r.results[0]["out_0_dram"]
```

```python
import numpy as np
import concourse.bass as bass
from concourse import mybir
from contextlib import ExitStack

F32 = mybir.dt.float32
F32R = mybir.dt.float32r
BF16 = mybir.dt.bfloat16
I32 = mybir.dt.int32
ALU = mybir.AluOpType
ACT = mybir.ActivationFunctionType
AX = mybir.AxisListType

P = 128
D = 128
NB, SEQ = 16, 256
NT = NB * SEQ // P
NH, DK = 16, 64
NPAIR = NH // 2
NE, FF = 8, 512
CAP = 256
SLOTS = NE * CAP
NI = FF // P
GT = 8
NG = NT // GT
BT = SEQ // P
EPS = 1e-5
SCALE = 1.0 / float(np.sqrt(DK))
NOSLOT = 2 * SLOTS


NV = 4 * BT
ROW_RES, ROW_ID, ROW_WT, ROW = D, 2 * D, 2 * D + 1, 2 * D + 2
WAIT_X, WAIT_ROWS, WAIT_X1, WAIT_NORM = 5, (11, 8), 10, 3
NOTOK = 2 * NT * P


def macaron_kernel(nc, x, w_qT, w_kT, w_v, w_o, gate, gamma, beta, wi, wo, ident_in, before_in, ebase_in, rev_in,
                   noslot_in, tokid_in, empty_in, out):
    ctx = ExitStack()
    with ctx:
        def sb(name, shape, dt=F32):
            return ctx.enter_context(nc.sbuf_tensor(name, shape, dt))

        def sem(name):
            return ctx.enter_context(nc.semaphore(name))

        X = sb("X", [P, NT, D])
        ident = sb("ident", [P, P])
        before = sb("before", [P, P], BF16)
        ones = sb("ones", [P, P], BF16)
        tri_f = sb("tri_f", [P, P])
        ebase = sb("ebase", [P, NE])
        rev = sb("rev", [P, NE])
        noslot = sb("noslot", [P, GT])
        gcol = sb("gcol", [P, 1])
        bcol = sb("bcol", [P, 1])
        gateT = sb("gateT", [P, NE])
        mhalf = sb("mhalf", [P, 2 * GT])
        spare = sb("spare", [P, 1])
        wqk = sb("wqk", [P, 2 * NPAIR * D])
        wqT, wkT = [wqk[:, i * NPAIR * D:(i + 1) * NPAIR * D].rearrange("p (a d) -> p a d", a=NPAIR) for i in range(2)]
        wv = sb("wv", [P, NH * DK])
        wvh = sb("wvh", [P, NH * DK], F32R)
        wvl = sb("wvl", [P, NH * DK], F32R)
        woh = sb("woh", [P, NPAIR, D], F32R)
        wol = sb("wol", [P, NPAIR, D], F32R)
        ah = sb("ah", [P, NH, D], F32R)
        al = sb("al", [P, NH, D], F32R)
        shared = [sb(f"shared{q}", [P, GT * ROW]) for q in range(NG)]

        class Routing:

            def __init__(self, f, n, ring):
                self.n, self.ring = n, ring
                small = ("mean", "diff", "m2", "var", "amul", "lmax",
                         "cmax", "rank", "base", "keep", "den", "rden", "d1", "d2", "d3")
                wide = ("dlt", "exl", "cand", "hotf", "lg", "rkp", "rk", "rsel", "bsel")
                self.tiles = {k: [sb(f"r{f}_{k}{q}", [P, n]) for q in range(ring)] for k in small}
                for k in wide:
                    self.tiles[k] = [sb(f"r{f}_{k}{q}", [P, n, NE]) for q in range(ring)]
                self.tiles["vars"] = [sb(f"r{f}_vars{q}", [P, 2 * n]) for q in range(ring)]
                self.tiles["rstd"] = [sb(f"r{f}_rstd{q}", [P, 2 * n]) for q in range(ring)]
                self.tiles["st"] = [sb(f"r{f}_st{q}", [P, n, 6]) for q in range(ring)]
                self.tiles["cadd"] = [sb(f"r{f}_cadd{q}", [P, n]) for q in range(ring)]
                self.tiles["tot"] = [sb(f"r{f}_tot{q}", [P, NE]) for q in range(ring)]
                self.tiles["hot"] = [sb(f"r{f}_hot{q}", [P, n, NE], BF16) for q in range(ring)]
                self.tiles["dest"] = [sb(f"r{f}_dest{q}", [P, n], I32) for q in range(ring)]
                self.tiles["tokT"] = [sb(f"r{f}_tokT", [P, n, P])] * ring
                self.tiles["row"] = ([t[:].rearrange("p (n r) -> p n r", r=ROW) for t in shared] if f == 0 else
                                     [sb(f"r{f}_row{q}", [P, n, ROW]) for q in range(ring)])
                self.seen = sb(f"r{f}_seen", [P, NE])

            def __call__(self, name, i):
                return self.tiles[name][i if self.ring > 1 else 0]
        rt = [Routing(0, GT, NG), Routing(1, BT, 1)]
        wos = rt[0]("tokT", 0)[:]
        tokid = sb("tokid", [P, NT])
        empty = sb("empty", [P, 4, ROW])
        ewi = [X[:, e * NI:(e + 1) * NI, :].rearrange("p i j -> p (i j)") for e in range(NE)]
        ewi_hi = [sb(f"ewi_hi{e}", [P, FF], F32R) for e in range(NE)]
        ewi_lo = [sb(f"ewi_lo{e}", [P, FF], F32R) for e in range(NE)]
        ewo = [sb(f"ewo{e}", [P, NI, D]) for e in range(NE)]
        ein = [wqk[:, i * 2 * ROW:(i + 1) * 2 * ROW].rearrange("p (c r) -> p c r", c=2) for i in range(3)] + \
            [sb("ein3", [P, 2, ROW])]
        einT = wqk[:, 6 * ROW:6 * ROW + CAP]
        eTh = [sb(f"eTh{i}", [P, CAP], F32R) for i in range(2)]
        eTl = [sb(f"eTl{i}", [P, CAP], F32R) for i in range(2)]
        ehT = [shared[2 + i][:, 0:NI * CAP].rearrange("p (i c) -> p i c", i=NI) for i in range(2)]
        eid = [sb(f"eid{i}", [P, 2], I32) for i in range(2)]
        eres = [sb(f"eres{i}", [P, 2, D]) for i in range(2)]
        c_st = sb("c_st", [P, BT, 6])
        c_mean, c_diff, c_m2, c_var, c_vare, c_rs, c_mul, c_add = [
            sb(f"c_{k}", [P, BT]) for k in ("mean", "diff", "m2", "var", "vare", "rs", "mul", "add")]

        def behind(q, k):
            at0 = NI * CAP + k * BT * D
            return shared[q][:, at0:at0 + BT * D].rearrange("p (t d) -> p t d", d=D)
        x1 = [behind(2, i) for i in range(2)]
        x1y = [behind(2, 2 + i) for i in range(2)]
        ya, x2, oT = behind(3, 0), behind(3, 1), behind(3, 2)
        yTh = [sb(f"yTh{i}", [P, SEQ], F32R) for i in range(2)]
        yTl = [sb(f"yTl{i}", [P, SEQ], F32R) for i in range(2)]
        Gh = [sb(f"Gh{i}", [P, 2 * SEQ], F32R) for i in range(2)]
        Gl = [sb(f"Gl{i}", [P, 2 * SEQ], F32R) for i in range(2)]
        V = X[:, 0:16, :].rearrange("p (t c) d -> p t (c d)", t=BT)
        mx = [sb(f"mx{i}", [P, 4]) for i in range(4)]
        nbias = [sb(f"nbias{i}", [P, 4]) for i in range(4)]
        sums = [sb(f"sums{i}", [P, 4]) for i in range(4)]
        rsum = [sb(f"rsum{i}", [P, 4]) for i in range(4)]
        prob = [shared[i // 2][:, (i % 2) * 4 * SEQ:(i % 2 + 1) * 4 * SEQ]
                .rearrange("p (c h k) -> p c h k", c=2, h=2) for i in range(4)]
        probT = [[X[:, 16 + 8 * i + 4 * h:20 + 8 * i + 4 * h, :].rearrange("p (j c) d -> p j (c d)", j=2)
                  for h in range(2)] for i in range(2)]
        zh = sb("zh", [P, NPAIR, SEQ], F32R)
        zl = sb("zl", [P, NPAIR, SEQ], F32R)
        zf = [sb(f"zf{i}", [P, SEQ]) for i in range(2)]
        SC = [[ctx.enter_context(nc.psum_tensor(f"SC{i}{c}", [P, 512], F32)) for c in range(2)] for i in range(2)]
        PT = [ctx.enter_context(nc.psum_tensor(f"PT{h}", [P, 512], F32)) for h in range(2)]
        PJ = ctx.enter_context(nc.psum_tensor("PJ", [P, 512], F32))
        Z = ctx.enter_context(nc.psum_tensor("Z", [P, 512], F32))
        disp = [nc.dram_tensor(f"disp{f}", [SLOTS, ROW], F32, kind="Internal").ap() for f in range(2)]
        x1_dram = nc.dram_tensor("x1_dram", [NT * P, D], F32, kind="Internal").ap()

        x_in = [sem(f"x_in{g}") for g in range(NG)]
        const_in, watt_in, consts = sem("const_in"), sem("watt_in"), sem("consts")
        before_ready, empty_in_done = sem("before_ready"), sem("empty_in_done")
        disp_emptied = [sem(f"disp_emptied{f}") for f in range(2)]
        a_ps, a_hi, a_lo, wv_hi, wv_lo = sem("a_ps"), sem("a_hi"), sem("a_lo"), sem("wv_hi"), sem("wv_lo")
        R = []
        for f in range(2):
            R.append({k: sem(f"f{f}_{k}") for k in (
                "stats", "var_ready", "rstd_ready", "tok_done", "tT_ps", "tT_ready", "logit_ps",
                "delta_ready", "exl_ready", "hot_ready", "hots", "rank_ps", "seen_done", "final", "dest_ready",
                "scattered", "first", "x_done", "stored", "logit_read", "rank_read", "aff", "id_set")})
        ein_in, ein_ps, ein_ready = [sem(f"ein_in{i}") for i in range(4)], sem("ein_ps"), sem("ein_ready")
        ew_in = [sem(f"ew_in{e}") for e in range(NE)]
        up_ps, gelu_done, down_ps, eres_ready = sem("up_ps"), sem("gelu_done"), sem("down_ps"), sem("eres_ready")
        eres_out = [sem(f"eres_out{i}") for i in range(2)]
        x1_in = [sem(f"x1_in{i}") for i in range(2)]
        ein_read, ein_hi, ewi_rounded, ewi_split = [sem(k) for k in ("ein_read", "ein_hi", "ewi_rounded", "ewi_split")]
        eid_ready, c_aff = sem("eid_ready"), sem("c_aff")
        c_stats, c_rstd, c_chain = sem("c_stats"), sem("c_rstd"), sem("c_chain")
        ya_ready, x_plus_ya = sem("ya_ready"), sem("x_plus_ya")
        yT_ps, yT_hi, yT_lo = sem("yT_ps"), sem("yT_hi"), sem("yT_lo")
        g_ps, g_hi, g_lo = sem("g_ps"), sem("g_hi"), sem("g_lo")
        v_ps, v_ready = sem("v_ps"), sem("v_ready")
        scores_ps, max_done, bias_ready = sem("scores_ps"), sem("max_done"), sem("bias_ready")
        exp_done, rsum_ready, prob_ready = sem("exp_done"), sem("rsum_ready"), sem("prob_ready")
        pT_ps, pT_even, pT_odd = sem("pT_ps"), sem("pT_even"), sem("pT_odd")
        z_ps, z_ready = sem("z_ps"), sem("z_ready")
        o_ps, oT_ready, o_back_ps, o_added = sem("o_ps"), sem("oT_ready"), sem("o_back_ps"), sem("o_added")
        z_lo, wo_in, wo_hi, wo_lo = sem("z_lo"), sem("wo_in"), sem("wo_hi"), sem("wo_lo")
        table_loaded = sem("table_loaded")

        block = ctx.enter_context(nc.Block())

        ABANK = [SC[1][0], SC[1][1], PT[0], PT[1]]

        def heads4(t, q):
            return t[:, 8 * (q // 2):8 * (q // 2) + 8, :].rearrange("p (k two) d -> p k two d", two=2)[:, :, q % 2, :]

        def four(bank):
            return bank[:].rearrange("p (k d) -> p k d", k=4)

        def bc(ap, n):
            return ap.unsqueeze(2).to_broadcast([P, ap.shape[1], n])


        N_VAR = 7
        N_FINAL = 11

        def dve_var(dve, stats, chain_sem, mean, diff, m2, vare, var, base):
            k = base
            nc.vector.tensor_tensor(mean, stats[:, :, 1], stats[:, :, 4], ALU.add).then_inc(chain_sem, 1)
            nc.vector.tensor_tensor(diff, stats[:, :, 1], stats[:, :, 4], ALU.subtract).then_inc(chain_sem, 1)
            nc.vector.tensor_tensor(m2, stats[:, :, 2], stats[:, :, 5], ALU.add).then_inc(chain_sem, 1)
            dve.wait_ge(chain_sem, k + 2)
            nc.vector.scalar_tensor_tensor(diff, diff, 0.25, diff, ALU.mult, ALU.mult).then_inc(chain_sem, 1)
            nc.vector.tensor_scalar(mean, mean, 0.5, None, ALU.mult).then_inc(chain_sem, 1)
            dve.wait_ge(chain_sem, k + 4)
            nc.vector.scalar_tensor_tensor(var, m2, 1.0 / D, diff, ALU.mult, ALU.add).then_inc(chain_sem, 1)
            dve.wait_ge(chain_sem, k + 6)
            nc.vector.tensor_scalar(vare, var, EPS, None, ALU.add).then_inc(chain_sem, 1)

        def is_first(i, n=1):
            return isinstance(i, int) and i < n

        def route_stats(dve, f, i, xs):
            r, s, n = rt[f], R[f], rt[f].n
            for j in range(n):
                ins = nc.vector.bn_stats(r("st", i)[:, j, :], xs[:, j, :])
            ins.then_inc(s["first"], 1)
            dve.wait_ge(s["first"], i + 1)
            b, vars_ = i * N_VAR, r("vars", i)
            dve_var(dve, r("st", i), s["stats"], r("mean", i)[:], r("diff", i)[:], r("m2", i)[:], vars_[:, 0:n],
                    r("var", i)[:], b)
            dve.wait_ge(s["stats"], b + N_VAR)
            nc.vector.scalar_tensor_tensor(vars_[:, n:2 * n], vars_[:, 0:n], EPS, r("var", i)[:], ALU.mult,
                                           ALU.add).then_inc(s["var_ready"], 1)

        def route_rstd(pool, f, i):
            r, s = rt[f], R[f]
            pool.wait_ge(s["var_ready"], i + 1)
            nc.gpsimd.tensor_tensor(r("rstd", i)[:], r("vars", i)[:], mhalf[:, 0:2 * r.n], ALU.pow) \
                .then_inc(s["rstd_ready"], 1)

        def route_norm(dve, f, i, xs, ids):
            r, s, n = rt[f], R[f], rt[f].n
            row = r("row", i)
            mean, rs, rst = r("mean", i), r("rstd", i)[:, 0:n], r("rstd", i)[:, n:2 * n]
            amul, cadd = r("amul", i), r("cadd", i)
            dve.wait_ge(s["rstd_ready"], i + 1)
            nc.vector.tensor_scalar(amul[:], rs, 0.5, 1.0, ALU.mult, ALU.add).then_inc(s["aff"], 1)
            nc.vector.scalar_tensor_tensor(cadd[:], rs, -0.5, mean[:], ALU.mult, ALU.mult).then_inc(s["aff"], 1)
            if r.ring == 1 and not is_first(i):
                dve.wait_ge(s["scattered"], i * n * 16)
                dve.wait_ge(s["stored"], i * 16)
            for j in range(n):
                ins = nc.vector.tensor_scalar(row[:, j, 0:D], xs[:, j, :], mean[:, j:j + 1], rst[:, j:j + 1],
                                              ALU.subtract, ALU.mult)
            ins.then_inc(s["tok_done"], 1)
            nc.vector.tensor_copy(row[:, :, ROW_ID], ids).then_inc(s["id_set"], 1)

        def read_logits(dve, f, i, logits):
            dve.wait_ge(R[f]["logit_ps"], i + 1)
            nc.vector.tensor_copy(rt[f]("lg", i)[:], logits).then_inc(R[f]["logit_read"], 1)

        def route_pick(dve, f, i):
            r, s, n = rt[f], R[f], rt[f].n
            b = i * 4
            lg, cand, hotf = r("lg", i)[:], r("cand", i)[:], r("hotf", i)[:]
            dve.wait_ge(s["logit_read"], i + 1)
            nc.vector.tensor_reduce(r("lmax", i)[:], lg, AX.X, ALU.max).then_inc(s["hots"], 1)
            dve.wait_ge(s["hots"], b + 1)
            nc.vector.tensor_tensor(r("dlt", i)[:], lg, bc(r("lmax", i)[:], NE), ALU.subtract) \
                .then_inc(s["delta_ready"], 1)
            dve.wait_ge(s["delta_ready"], i + 1)
            nc.vector.scalar_tensor_tensor(cand, r("dlt", i)[:], 0.0, rev[:].unsqueeze(1).to_broadcast([P, n, NE]),
                                           ALU.is_ge, ALU.mult).then_inc(s["hots"], 1)
            dve.wait_ge(s["hots"], b + 2)
            nc.vector.tensor_reduce(r("cmax", i)[:], cand, AX.X, ALU.max).then_inc(s["hots"], 1)
            dve.wait_ge(s["hots"], b + 3)
            nc.vector.tensor_tensor(hotf, cand, bc(r("cmax", i)[:], NE), ALU.is_equal).then_inc(s["hots"], 1)
            dve.wait_ge(s["hots"], b + 4)
            nc.vector.tensor_copy(r("hot", i)[:], hotf).then_inc(s["hot_ready"], 1)

        def read_ranks(dve, f, i, ranks):
            r, n = rt[f], rt[f].n
            dve.wait_ge(R[f]["rank_ps"], i + 1)
            nc.vector.tensor_copy(r("rkp", i)[:], ranks[:, 0:n, :])
            nc.vector.tensor_copy(r("tot", i)[:], ranks[:, n, :]).then_inc(R[f]["rank_read"], 1)

        def route_final(dve, f, i):
            r, s, n = rt[f], R[f], rt[f].n
            b = i * N_FINAL
            fin, hotf, row = s["final"], r("hotf", i)[:], r("row", i)
            tt, ts, stt = nc.vector.tensor_tensor, nc.vector.tensor_scalar, nc.vector.scalar_tensor_tensor
            tt(r("bsel", i)[:], hotf, ebase[:].unsqueeze(1).to_broadcast([P, n, NE]), ALU.mult).then_inc(fin, 1)
            dve.wait_ge(s["exl_ready"], i + 1)
            nc.vector.tensor_reduce(r("den", i)[:], r("exl", i)[:], AX.X, ALU.add).then_inc(fin, 1)
            if is_first(i):
                dve.wait_ge(consts, 4)
            else:
                dve.wait_ge(s["seen_done"], i)
            dve.wait_ge(s["rank_read"], i + 1)
            tt(r("rk", i)[:], r("rkp", i)[:], r.seen[:].unsqueeze(1).to_broadcast([P, n, NE]), ALU.add).then_inc(fin, 1)
            dve.wait_ge(fin, b + 3)
            tt(r.seen[:], r("tot", i)[:], r.seen[:], ALU.add).then_inc(s["seen_done"], 1)
            tt(r("rsel", i)[:], r("rk", i)[:], hotf, ALU.mult).then_inc(fin, 1)
            nc.vector.tensor_reduce(r("base", i)[:], r("bsel", i)[:], AX.X, ALU.add).then_inc(fin, 1)
            nc.vector.reciprocal(r("rden", i)[:], r("den", i)[:]).then_inc(fin, 1)
            dve.wait_ge(fin, b + 4)
            nc.vector.tensor_reduce(r("rank", i)[:], r("rsel", i)[:], AX.X, ALU.add).then_inc(fin, 1)
            dve.wait_ge(fin, b + 7)
            ts(r("keep", i)[:], r("rank", i)[:], float(CAP), None, ALU.is_lt).then_inc(fin, 1)
            tt(r("d1", i)[:], r("rank", i)[:], r("base", i)[:], ALU.add).then_inc(fin, 1)
            dve.wait_ge(fin, b + 9)
            tt(r("d2", i)[:], r("d1", i)[:], noslot[:, 0:n], ALU.subtract).then_inc(fin, 1)
            stt(row[:, :, ROW_WT], r("keep", i)[:], 0.5, r("rden", i)[:], ALU.mult, ALU.mult).then_inc(s["id_set"], 1)
            dve.wait_ge(fin, b + 10)
            tt(r("d3", i)[:], r("d2", i)[:], r("keep", i)[:], ALU.mult).then_inc(fin, 1)
            dve.wait_ge(s["id_set"], 2 * i + 2)
            dve.wait_ge(fin, b + 11)
            tt(r("dest", i)[:], r("d3", i)[:], noslot[:, 0:n], ALU.add).then_inc(s["dest_ready"], 1)

        def route_scatter(pool, f, i):
            r, s = rt[f], R[f]
            for j in range(r.n):
                nc.gpsimd.indirect_dma_start(
                    out=disp[f][:, :], out_offset=bass.IndirectOffsetOnAxis(r("dest", i)[:, j:j + 1], 0),
                    in_=r("row", i)[:, j, :], in_offset=None, bounds_check=SLOTS - 1,
                    oob_is_err=False).then_inc(s["scattered"], 16)

        def pe_ranks(f, i, ps):
            r, n = rt[f], rt[f].n
            hot = r("hot", i)
            for j in range(n + 1):
                earlier = list(range(min(j, n)))
                if j < n:
                    ins = nc.tensor.matmul(ps[:, j, :], before[:], hot[:, j, :], start=True, stop=not earlier)
                for k in earlier:
                    ins = nc.tensor.matmul(ps[:, j, :], ones[:], hot[:, k, :], start=j == n and k == 0,
                                           stop=k == earlier[-1])
            return ins

        UPS = [[SC[1][0], SC[1][1]], [PT[0], PT[1]]]
        DNS = [PJ, Z]

        def sp_rows(sp, E):
            if E >= 4:
                sp.wait_ge(eres_ready, 2 * (E - 3))
            e = E % NE
            sp.dma_start(ein[E % 4][:], disp[E // NE][e * CAP:(e + 1) * CAP, :].rearrange("(c p) d -> p c d", p=P)) \
                .then_inc(ein_in[E % 4], 16)

        def pe_expert_in(pe, E):
            pe.wait_ge(ein_in[E % 4], 16 * (E // 4 + 1))
            if E >= 2:
                pe.wait_ge(ein_read, E - 1)
            for c in range(2):
                ins = nc.tensor.transpose(SC[0][E % 2][:, c * P:(c + 1) * P], ein[E % 4][:, c, 0:D], ident[:])
            ins.then_inc(ein_ps, 1)

        def pe_expert_up(pe, E):
            if E < NE:
                pe.wait_ge(ewi_split, E + 1)
                pe.wait_ge(ew_in[E], 32)
            pe.wait_ge(ein_ready, E + 1)
            if E >= 2:
                pe.wait_ge(gelu_done, 2 * E - 2)
            for i in range(NI):
                o = UPS[E % 2][i // 2][:, (i % 2) * CAP:(i % 2 + 1) * CAP]
                hi, lo = ewi_hi[E % NE][:, i * P:(i + 1) * P], ewi_lo[E % NE][:, i * P:(i + 1) * P]
                nc.tensor.matmul(o, hi, eTh[E % 2][:], start=True, stop=False)
                nc.tensor.matmul(o, lo, eTh[E % 2][:], start=False, stop=False)
                ins = nc.tensor.matmul(o, hi, eTl[E % 2][:], start=False, stop=True)
                if i % 2:
                    ins.then_inc(up_ps, 1)

        def pe_expert_down(pe, E):
            pe.wait_ge(gelu_done, 2 * E + 2)
            for c in range(2):
                if E >= 1:
                    pe.wait_ge(eres_ready, 2 * E + c - 1)
                for i in range(NI):
                    ins = nc.tensor.matmul(DNS[c][:, 0:D], ehT[E % 2][:, i, c * P:(c + 1) * P],
                                           ewo[E % NE][:, i, :], start=i == 0, stop=i == NI - 1)
                ins.then_inc(down_ps, 1)

        def act_expert(act, E):
            for u in range(2):
                act.wait_ge(up_ps, 2 * E + u + 1)
                if u == 0 and E >= 2:
                    act.wait_ge(down_ps, 2 * E - 2)
                nc.scalar.activation(ehT[E % 2][:, 2 * u:2 * u + 2, :].rearrange("p i c -> p (i c)"),
                                     UPS[E % 2][u][:], ACT.Gelu).then_inc(gelu_done, 1)

        def dve_expert_in(dve, E):
            dve.wait_ge(ein_ps, E + 1)
            if E >= 1:
                dve.wait_ge(ein_ready, E)
            nc.vector.tensor_scalar(einT[:], SC[0][E % 2][:, 0:CAP], gcol[:], bcol[:],
                                    ALU.mult, ALU.add).then_inc(ein_read, 1)
            if E >= 2:
                dve.wait_ge(up_ps, 2 * E - 2)
            dve.wait_ge(ein_read, E + 1)
            nc.vector.tensor_copy(eTh[E % 2][:], einT[:]).then_inc(ein_hi, 1)
            dve.wait_ge(ein_hi, E + 1)
            nc.vector.tensor_tensor(eTl[E % 2][:], einT[:], eTh[E % 2][:].bitcast(F32), ALU.subtract) \
                .then_inc(ein_ready, 1)

        def dve_expert_out(dve, E):
            rows, par = ein[E % 4], E % 2
            if E >= 2:
                dve.wait_ge(eres_out[par], 32 * (E // 2))
            nc.vector.tensor_copy(eid[par][:], rows[:, :, ROW_ID]).then_inc(eid_ready, 1)
            for c in range(2):
                dve.wait_ge(down_ps, 2 * E + c + 1)
                nc.vector.scalar_tensor_tensor(
                    eres[par][:, c, :], DNS[c][:, 0:D], rows[:, c, ROW_WT:ROW_WT + 1],
                    rows[:, c, ROW_RES:ROW_RES + D], ALU.mult, ALU.add).then_inc(eres_ready, 1)

        def pool_expert_out(pool, E, target):
            pool.wait_ge(eid_ready, E + 1)
            for c in range(2):
                pool.wait_ge(eres_ready, 2 * E + c + 1)
                nc.gpsimd.indirect_dma_start(
                    out=target, out_offset=bass.IndirectOffsetOnAxis(eid[E % 2][:, c:c + 1], 0),
                    in_=eres[E % 2][:, c, :], in_offset=None, bounds_check=NT * P - 1,
                    oob_is_err=False).then_inc(eres_out[E % 2], 16)

        def experts(f, take_in, up, down):
            E0 = NE * f
            take_in(E0)
            take_in(E0 + 1)
            up(E0)
            for E in range(E0, E0 + NE):
                if E + 2 < E0 + NE:
                    take_in(E + 2)
                if E + 1 < E0 + NE:
                    up(E + 1)
                down(E)

        def sp_experts(sp, f):
            sp.wait_ge(R[f]["scattered"], NT * 16)
            for E in range(NE * f, NE * f + NE):
                sp_rows(sp, E)

        x1t = x1_dram.rearrange("(t p) d -> p t d", p=P)
        xt = x.rearrange("b (t p) d -> p (b t) d", p=P)
        ot = out.rearrange("b (t p) d -> p (b t) d", p=P)

        VPS = Z[:, SEQ:2 * SEQ]
        HALF = PJ[:, 0:SEQ]
        MIDDLE = {0: ("logit", -2), 2: ("rank", -2), 3: ("o", -1), 4: ("o_back", -1), 5: ("yT", 1), 7: ("tT", -1)}
        PJ_READ = {"g": (g_lo, NPAIR), "rank": (R[1]["rank_read"], 1), "o": (oT_ready, 1),
                   "o_back": (o_added, 1), "yT": (yT_lo, 1), "tT": (R[1]["tT_ready"], 1),
                   "logit": (R[1]["logit_read"], 1)}
        O_TAIL = {0: range(5), 1: (5,), 2: (6,), 3: (7,)}

        def o_bank(b):
            return SC[0][0][:, 0:SEQ] if isinstance(b, int) and b == NB else HALF

        def valid(b):
            return not isinstance(b, int) or 0 <= b < NB

        def at(b, p):
            return b * NPAIR + p

        def run(eng, batch):
            batch(0, 0)
            batch(1, 1)
            with eng.Fori(1, NB // 2 - 1) as k:
                batch(2 * k, 0)
                batch(2 * k + 1, 1)
            batch(NB - 2, 0)
            batch(NB - 1, 1)
            batch(NB, 0)
            batch(NB + 1, 1)

        def seq(b):
            return slice(BT * b, BT * b + BT) if isinstance(b, int) else bass.ds(BT * b, BT)

        def back(b, p, k):
            return (b, p - k) if p >= k else (b - 1, p - k + NPAIR)

        def fwd(b, p):
            return (b, p + 1) if p + 1 < NPAIR else (b + 1, 0)

        @block.sync
        def _(sp):
            for g in range(NG):
                sp.dma_start(X[:, g * GT:(g + 1) * GT, :], xt[:, g * GT:(g + 1) * GT, :]).then_inc(x_in[g], 16)

            def empty_slots(f):
                for q in range(SLOTS // P // 4):
                    sp.dma_start(disp[f][q * 4 * P:(q + 1) * 4 * P, :].rearrange("(r p) d -> p r d", p=P),
                                 empty[:]).then_inc(disp_emptied[f], 16)
            sp.wait_ge(empty_in_done, 16)
            empty_slots(0)
            sp.dma_start(wqT[:], w_qT.rearrange("(a p) d -> p a d", p=P)).then_inc(watt_in, 16)
            sp.dma_start(wkT[:], w_kT.rearrange("(a p) d -> p a d", p=P)).then_inc(watt_in, 16)
            sp.dma_start(wv[:], w_v).then_inc(watt_in, 16)
            for e in range(NE):
                sp.dma_start(ewo[e][:], wo[e].rearrange("(i p) d -> p i d", p=P)).then_inc(ew_in[e], 16)
            for g in range(NG):
                sp.wait_ge(R[0]["x_done"], g + 1)
                sp.dma_start(x1t[:, g * GT:(g + 1) * GT, :], rt[0]("row", g)[:, :, ROW_RES:ROW_RES + D]) \
                    .then_inc(R[0]["stored"], 16)
            sp.wait_ge(R[0]["tok_done"], NG)
            for e in range(NE):
                sp.dma_start(ewi[e], wi[e]).then_inc(ew_in[e], 16)
            sp.wait_ge(R[0]["logit_ps"], NG)
            sp.dma_start(wos, w_o.rearrange("(a p) d -> p a d", p=P)).then_inc(wo_in, 16)
            sp.wait_ge(a_ps, 4)
            sp.wait_ge(R[0]["stored"], 16 * NG)
            sp_experts(sp, 0)
            empty_slots(1)
            for par in range(2):
                sp.wait_ge(eres_out[par], 16 * NE)

            def load_x1(b, par):
                if not is_first(b, 2):
                    sp.wait_ge(x_plus_ya, b - 1)
                sp.dma_start(x1[par][:], x1t[:, seq(b), :]).then_inc(x1_in[par], 16)

            def batch(b, par):
                if valid(b + 2):
                    load_x1(b + 2, par)
                if valid(b - 2):
                    sp.wait_ge(R[1]["x_done"], b - 1)
                    sp.dma_start(ot[:, seq(b - 2), :], rt[1]("row", 0)[:, :, ROW_RES:ROW_RES + D]) \
                        .then_inc(R[1]["stored"], 16)
            load_x1(0, 0)
            load_x1(1, 1)
            run(sp, batch)
            sp_experts(sp, 1)
            for par in range(2):
                sp.wait_ge(eres_out[par], 32 * NE)
            sp.wait_ge(R[1]["stored"], 16 * NB)

        @block.gpsimd
        def _(pool):
            nc.gpsimd.memset(mhalf[:], -0.5).then_inc(consts, 1)
            nc.gpsimd.memset(ones[:], 1.0).then_inc(consts, 1)
            nc.gpsimd.memset(rt[0].seen[:], 0.0).then_inc(consts, 1)
            nc.gpsimd.memset(rt[1].seen[:], 0.0).then_inc(consts, 1)
            pool.wait_ge(consts, 4)

            def scatter(g):
                pool.wait_ge(R[0]["x_done"], g + 1)
                pool.wait_ge(R[0]["dest_ready"], g + 1)
                route_scatter(pool, 0, g)
            for g in range(NG):
                route_rstd(pool, 0, g)
            pool.wait_ge(disp_emptied[0], 16 * (SLOTS // P // 4))
            for g in range(NG):
                scatter(g)
            pool.wait_ge(wv_hi, 1)
            nc.gpsimd.tensor_tensor(wvl[:], wv[:], wvh[:].bitcast(F32), ALU.subtract).then_inc(wv_lo, 1)
            pool.wait_ge(R[0]["stored"], 16 * NG)
            for e in range(NE):
                pool_expert_out(pool, e, x1_dram[:, :])
            pool.wait_ge(disp_emptied[1], 16 * (SLOTS // P // 4))

            def prep_rstd(b):
                pool.wait_ge(c_chain, N_VAR * (b + 1))
                nc.gpsimd.tensor_tensor(c_rs[:], c_vare[:], mhalf[:, 0:BT], ALU.pow).then_inc(c_rstd, 1)

            def batch(b, par):
                for p in range(NPAIR):
                    zb, zp = back(b, p, 4)
                    if valid(zb):
                        pool.wait_ge(z_ready, at(zb, zp) + 1)
                        nc.gpsimd.tensor_tensor(zl[:, zp, :], zf[zp % 2][:], zh[:, zp, :].bitcast(F32),
                                                ALU.subtract).then_inc(z_lo, 1)
                    if p == 6 and valid(b - 1):
                        route_rstd(pool, 1, b - 1)
                    pb, pp = back(b, p, 1)
                    if p == 3 and valid(b - 2):
                        pool.wait_ge(R[1]["x_done"], b - 1)
                        pool.wait_ge(R[1]["dest_ready"], b - 1)
                    if valid(pb):
                        pool.wait_ge(rsum_ready, at(pb, pp) + 1)
                        q = pp % 4
                        v = prob[q][:].rearrange("p c h k -> p (c h) k")
                        nc.gpsimd.tensor_tensor(v, v, bc(rsum[q][:], SEQ), ALU.mult).then_inc(prob_ready, 1)
                    if p == 2 and valid(b + 1):
                        prep_rstd(b + 1)
                    if p == 3 and valid(b - 2):
                        route_scatter(pool, 1, 0)
            prep_rstd(0)
            run(pool, batch)
            pool.wait_ge(R[1]["stored"], 16 * NB)
            for e in range(NE):
                pool_expert_out(pool, NE + e, out.rearrange("b s d -> (b s) d"))

        @block.scalar
        def _(act):
            for tile, source in ((ident, ident_in), (tri_f, before_in), (tokid, tokid_in), (gcol, gamma), (bcol, beta),
                                 (gateT, gate), (rev, rev_in), (ebase, ebase_in), (noslot, noslot_in)):
                act.dma_start(tile[:], source).then_inc(const_in, 16)
            act.dma_start(empty[:], empty_in).then_inc(empty_in_done, 16)
            act.wait_ge(consts, 4)

            def load_exp_table(k):
                if k > 1:
                    act.wait_ge(table_loaded, k - 1)
                nc.scalar.activation(spare[:], mhalf[:, 0:1], ACT.Exp).then_inc(table_loaded, 1)
            load_exp_table(1)
            act.wait_ge(const_in, 144)

            def route_tT(f, i, banks, width):
                r, s = rt[f], R[f]
                for k, bank in enumerate(banks):
                    act.wait_ge(s["tT_ps"], len(banks) * i + k + 1)
                    nc.scalar.activation(r("tokT", i)[:].rearrange("p n q -> p (n q)")[:, k * width:(k + 1) * width],
                                         bank[:, 0:width], ACT.Identity, bias=bcol[:], scale=gcol[:]) \
                        .then_inc(s["tT_ready"], 1)

            def route_exp(f, i):
                r, s = rt[f], R[f]
                act.wait_ge(s["delta_ready"], i + 1)
                nc.scalar.activation(r("exl", i)[:], r("dlt", i)[:], ACT.Exp).then_inc(s["exl_ready"], 1)

            def residual(f, i, xs):
                amul, cadd, row = rt[f]("amul", i), rt[f]("cadd", i), rt[f]("row", i)
                act.wait_ge(R[f]["aff"], 2 * i + 2)
                for j in range(rt[f].n):
                    ins = nc.scalar.activation(row[:, j, ROW_RES:ROW_RES + D], xs[:, j, :], ACT.Identity,
                                               bias=cadd[:, j:j + 1], scale=amul[:, j:j + 1])
                ins.then_inc(R[f]["x_done"], 1)
            for g in range(NG):
                route_tT(0, g, [SC[0][0], SC[0][1]], 512)
                if g:
                    route_exp(0, g - 1)
                residual(0, g, X[:, g * GT:(g + 1) * GT, :])
            route_exp(0, NG - 1)
            act.wait_ge(watt_in, 48)
            nc.scalar.activation(wvh[:], wv[:], ACT.Copy).then_inc(wv_hi, 1)
            for q in range(4):
                act.wait_ge(a_ps, q + 1)
                nc.scalar.activation(heads4(ah, q), four(ABANK[q]), ACT.Copy).then_inc(a_hi, 1)
            for e in range(NE):
                act.wait_ge(ew_in[e], 32)
                nc.scalar.activation(ewi_hi[e][:], ewi[e], ACT.Copy).then_inc(ewi_rounded, 1)
            act.wait_ge(wo_in, 16)
            nc.scalar.activation(woh[:], wos, ACT.Copy).then_inc(wo_hi, 1)
            for E in range(NE):
                act_expert(act, E)

            def prep_hi(b, par):
                act.wait_ge(yT_ps, b + 1)
                nc.scalar.activation(yTh[par][:], HALF, ACT.Copy).then_inc(yT_hi, 1)

            def g_hi_part(b, p):
                act.wait_ge(g_ps, at(b, p) + 1)
                if not (isinstance(b, int) and at(b, p) < 2):
                    act.wait_ge(scores_ps, 2 * at(b, p) - 2)
                nc.scalar.activation(Gh[p % 2][:], PJ[:], ACT.Copy).then_inc(g_hi, 1)

            def exps(p, c):
                for h in range(2):
                    k = 2 * c + h
                    ins = nc.scalar.activation(
                        prob[p % 4][:, c, h, :], SC[p % 2][c][:, h * SEQ:(h + 1) * SEQ], ACT.Exp,
                        bias=nbias[p % 4][:, k:k + 1], scale=SCALE, accum_out=sums[p % 4][:, k:k + 1])
                ins.then_inc(exp_done, 1)

            def batch(b, par):
                for p in range(NPAIR):
                    zb, zp = back(b, p, 4)
                    if valid(zb):
                        act.wait_ge(z_ps, at(zb, zp) + 1)
                        if not is_first(zb):
                            act.wait_ge(o_ps, zb)
                        if not (isinstance(zb, int) and at(zb, zp) < 2):
                            act.wait_ge(z_lo, at(zb, zp) - 1)
                        nc.scalar.activation(zh[:, zp, :], Z[:, 0:SEQ], ACT.Copy)
                        nc.scalar.activation(zf[zp % 2][:], Z[:, 0:SEQ], ACT.Copy).then_inc(z_ready, 1)
                    nb, np_ = fwd(b, p)
                    if valid(nb):
                        g_hi_part(nb, np_)
                    pb, pp = back(b, p, 1)
                    if valid(pb):
                        act.wait_ge(bias_ready, at(pb, pp) + 1)
                        if not (isinstance(pb, int) and at(pb, pp) < 4):
                            act.wait_ge(pT_ps, 2 * at(pb, pp) - 6)
                        exps(pp, 0)
                    if valid(b):
                        act.wait_ge(v_ps, NV * b + p + 1)
                        nc.scalar.activation(V[:, p % BT, (p // BT) * SEQ:(p // BT + 1) * SEQ], VPS,
                                             ACT.Copy).then_inc(v_ready, 1)
                    if valid(pb):
                        exps(pp, 1)
                    if p == 3 and valid(b - 2):
                        residual(1, b - 2, x2)
                    if p == 3 and valid(b - 1):
                        act.wait_ge(o_ps, b)
                        nc.scalar.activation(oT.rearrange("p t d -> p (t d)"), o_bank(b), ACT.Copy) \
                            .then_inc(oT_ready, 1)
                    if p == 5 and valid(b + 1):
                        prep_hi(b + 1, 1 - par)
                    if p == 7 and valid(b - 1):
                        route_tT(1, b - 1, [HALF], SEQ)
                    tb, tp = back(b, p, 2)
                    if valid(tb):
                        act.wait_ge(pT_ps, 2 * at(tb, tp) + 1)
                        if not (isinstance(tb, int) and at(tb, tp) < 2):
                            act.wait_ge(z_ps, at(tb, tp) - 1)
                        nc.scalar.activation(probT[tp % 2][0].rearrange("p j q -> p (j q)"), PT[0][:],
                                             ACT.Copy).then_inc(pT_even, 1)
                    if p == 1 and valid(b - 2):
                        route_exp(1, b - 2)
            load_exp_table(2)
            prep_hi(0, 0)
            g_hi_part(0, 0)
            run(act, batch)
            for E in range(NE, 2 * NE):
                act_expert(act, E)

        @block.vector
        def _(dve):
            logits8 = PJ[:, 0:GT * NE].rearrange("p (n e) -> p n e", e=NE)
            ranks8 = Z[:, 0:(GT + 1) * NE].rearrange("p (n e) -> p n e", e=NE)

            def stats(g):
                dve.wait_ge(x_in[g], 16)
                route_stats(dve, 0, g, X[:, g * GT:(g + 1) * GT, :])

            def norm(g):
                route_norm(dve, 0, g, X[:, g * GT:(g + 1) * GT, :], tokid[:, g * GT:(g + 1) * GT])

            def pick(g):
                read_logits(dve, 0, g, logits8)
                route_pick(dve, 0, g)

            def final(g):
                read_ranks(dve, 0, g, ranks8)
                route_final(dve, 0, g)
            stats(0)
            stats(1)
            dve.wait_ge(const_in, 144)
            nc.vector.tensor_copy(before[:], tri_f[:]).then_inc(before_ready, 1)
            for stage, g in ((norm, 0), (stats, 2), (norm, 1), (pick, 0), (stats, 3), (final, 0), (norm, 2), (pick, 1),
                             (norm, 3), (final, 1), (pick, 2), (final, 2), (pick, 3), (final, 3)):
                stage(g)
            for q in range(4):
                dve.wait_ge(a_hi, q + 1)
                nc.vector.tensor_tensor(heads4(al, q), four(ABANK[q]), heads4(ah, q).bitcast(F32),
                                        ALU.subtract).then_inc(a_lo, 1)
            for e in range(NE):
                dve.wait_ge(ewi_rounded, e + 1)
                nc.vector.tensor_tensor(ewi_lo[e][:], ewi[e], ewi_hi[e][:].bitcast(F32), ALU.subtract) \
                    .then_inc(ewi_split, 1)
            dve.wait_ge(wo_hi, 1)
            nc.vector.tensor_tensor(wol[:], wos, woh[:].bitcast(F32), ALU.subtract).then_inc(wo_lo, 1)
            experts(0, lambda E: dve_expert_in(dve, E), lambda E: None, lambda E: dve_expert_out(dve, E))

            def prep_stats(b, par):
                dve.wait_ge(x1_in[par], 8 * (b - par) + 16)
                for j in range(BT):
                    ins = nc.vector.bn_stats(c_st[:, j, :], x1[par][:, j, :])
                ins.then_inc(c_stats, 1)
                dve.wait_ge(c_stats, b + 1)
                dve_var(dve, c_st, c_chain, c_mean[:], c_diff[:], c_m2[:], c_vare[:], c_var[:],
                        b * N_VAR)

            def prep_norm(b, par):
                dve.wait_ge(c_rstd, b + 1)
                nc.vector.tensor_scalar(c_mul[:], c_rs[:], 1.0, None, ALU.add).then_inc(c_aff, 1)
                nc.vector.scalar_tensor_tensor(c_add[:], c_rs[:], -1.0, c_mean[:], ALU.mult, ALU.mult) \
                    .then_inc(c_aff, 1)
                if not is_first(b):
                    dve.wait_ge(yT_ps, b)
                for j in range(BT):
                    ins = nc.vector.tensor_scalar(ya[:, j, :], x1[par][:, j, :], c_mean[:, j:j + 1],
                                                  c_rs[:, j:j + 1], ALU.subtract, ALU.mult)
                ins.then_inc(ya_ready, 1)

            def prep_x1y(b, par):
                if not is_first(b, 2):
                    dve.wait_ge(o_added, b - 1)
                dve.wait_ge(c_aff, 2 * b + 2)
                for j in range(BT):
                    ins = nc.vector.tensor_scalar(x1y[par][:, j, :], x1[par][:, j, :], c_mul[:, j:j + 1],
                                                  c_add[:, j:j + 1], ALU.mult, ALU.add)
                ins.then_inc(x_plus_ya, 1)

            def prep_lo(b, par):
                dve.wait_ge(yT_hi, b + 1)
                nc.vector.tensor_tensor(yTl[par][:], HALF, yTh[par][:].bitcast(F32),
                                        ALU.subtract).then_inc(yT_lo, 1)

            def g_lo_part(b, p):
                dve.wait_ge(g_hi, at(b, p) + 1)
                nc.vector.tensor_tensor(Gl[p % 2][:], PJ[:], Gh[p % 2][:].bitcast(F32), ALU.subtract) \
                    .then_inc(g_lo, 1)

            def ranks_from_pj(b):
                read_ranks(dve, 1, b, PJ[:, 0:(BT + 1) * NE].rearrange("p (n e) -> p n e", e=NE))

            def batch(b, par):
                for p in range(NPAIR):
                    nb, np_ = fwd(b, p)
                    if valid(nb):
                        g_lo_part(nb, np_)
                    if valid(b):
                        g = at(b, p)
                        for c in range(2):
                            dve.wait_ge(scores_ps, 2 * g + c + 1)
                            ins = nc.vector.tensor_reduce(
                                mx[p % 4][:, 2 * c:2 * c + 2],
                                SC[p % 2][c][:].rearrange("p (h k) -> p h k", h=2), AX.X, ALU.max)
                        ins.then_inc(max_done, 1)
                        dve.wait_ge(max_done, g + 1)
                        nc.vector.tensor_scalar(nbias[p % 4][:], mx[p % 4][:], -SCALE, None,
                                                ALU.mult).then_inc(bias_ready, 1)
                    pb, pp = back(b, p, 1)
                    if valid(pb):
                        dve.wait_ge(exp_done, 2 * at(pb, pp) + 2)
                        if not (isinstance(pb, int) and at(pb, pp) < 4):
                            dve.wait_ge(prob_ready, at(pb, pp) - 3)
                        nc.vector.reciprocal(rsum[pp % 4][:], sums[pp % 4][:]).then_inc(rsum_ready, 1)
                    if p == 3 and valid(b - 2):
                        route_final(dve, 1, b - 2)
                    if p == 3 and valid(b + 1):
                        prep_norm(b + 1, 1 - par)
                    if p == 2 and valid(b - 2) and valid(b):
                        ranks_from_pj(b - 2)
                    if p == 4 and valid(b - 1):
                        if not is_first(b - 1):
                            dve.wait_ge(R[1]["x_done"], b - 1)
                        dve.wait_ge(o_back_ps, b)
                        nc.vector.tensor_tensor(x2, HALF.rearrange("p (t d) -> p t d", d=D),
                                                x1y[1 - par], ALU.add).then_inc(o_added, 1)
                    if p == 5 and valid(b + 1):
                        prep_lo(b + 1, 1 - par)
                    if p == 0 and valid(b - 2):
                        read_logits(dve, 1, b - 2, PJ[:, 0:BT * NE].rearrange("p (n e) -> p n e", e=NE))
                    tb, tp = back(b, p, 2)
                    if valid(tb):
                        dve.wait_ge(pT_ps, 2 * at(tb, tp) + 2)
                        if not (isinstance(tb, int) and at(tb, tp) < 2):
                            dve.wait_ge(z_ps, at(tb, tp) - 1)
                        nc.vector.tensor_copy(probT[tp % 2][1].rearrange("p j q -> p (j q)"),
                                              PT[1][:]).then_inc(pT_odd, 1)
                    if p == 2 and valid(b - 2) and not valid(b):
                        ranks_from_pj(b - 2)
                    if p == 0 and valid(b - 2):
                        route_pick(dve, 1, b - 2)
                    if p == 1 and valid(b + 1):
                        prep_stats(b + 1, 1 - par)
                    if p == 4 and valid(b + 1):
                        prep_x1y(b + 1, 1 - par)
                    if p == 5 and valid(b - 1):
                        dve.wait_ge(o_added, b)
                        route_stats(dve, 1, b - 1, x2)
                    if p == 6 and valid(b - 1):
                        route_norm(dve, 1, b - 1, x2, tokid[:, seq(b - 1)])

            prep_stats(0, 0)
            prep_norm(0, 0)
            prep_x1y(0, 0)
            prep_lo(0, 0)
            g_lo_part(0, 0)
            run(dve, batch)
            experts(1, lambda E: dve_expert_in(dve, E), lambda E: None, lambda E: dve_expert_out(dve, E))

        @block.tensor
        def _(pe):
            def keep_busy(n, bank, columns):
                for _ in range(n):
                    nc.tensor.matmul(bank[:], columns[:, 0:P], columns, start=True, stop=True)
            pe.wait_ge(x_in[0], 16)
            keep_busy(WAIT_X, PT[0], X[:, 0:4, :].rearrange("p t d -> p (t d)"))
            pe.wait_ge(const_in, 144)
            pe.wait_ge(consts, 4)
            pe.wait_ge(before_ready, 1)
            r, s = rt[0], R[0]

            def transposes(g):
                pe.wait_ge(s["tok_done"], g + 1)
                if g:
                    pe.wait_ge(s["tT_ready"], 2 * g)
                for j in range(GT):
                    ins = nc.tensor.transpose(SC[0][j // 4][:, (j % 4) * P:(j % 4 + 1) * P],
                                              r("row", g)[:, j, 0:D], ident[:])
                    if j % 4 == 3:
                        ins.then_inc(s["tT_ps"], 1)

            def logits(g):
                if g:
                    pe.wait_ge(s["logit_read"], g)
                for j in range(GT):
                    if j % 4 == 0:
                        pe.wait_ge(s["tT_ready"], 2 * g + j // 4 + 1)
                    ins = nc.tensor.matmul(PJ[:, j * NE:(j + 1) * NE], r("tokT", g)[:, j, :], gateT[:],
                                           start=True, stop=True)
                ins.then_inc(s["logit_ps"], 1)

            def ranks(g):
                pe.wait_ge(s["hot_ready"], g + 1)
                if g:
                    pe.wait_ge(s["rank_read"], g)
                pe_ranks(0, g, Z[:, 0:(GT + 1) * NE].rearrange("p (n e) -> p n e", e=NE)).then_inc(s["rank_ps"], 1)
            transposes(0)
            for g in range(NG):
                logits(g)
                if g + 1 < NG:
                    transposes(g + 1)
                ranks(g)
            pe.wait_ge(watt_in, 48)
            for q in range(4):
                for k in range(4):
                    h = 8 * (q // 2) + 2 * k + q % 2
                    half = slice(DK * (h % 2), DK * (h % 2) + DK)
                    ins = nc.tensor.matmul(ABANK[q][:, k * D:(k + 1) * D], wqT[half, h // 2, :],
                                           wkT[half, h // 2, :], start=True, stop=True)
                ins.then_inc(a_ps, 1)
            pe.wait_ge(a_lo, 4)
            pe.wait_ge(R[0]["rank_read"], NG)
            pe.wait_ge(ew_in[0], 32)
            some_weights = ewo[0][:].rearrange("p i d -> p (i d)")
            keep_busy(WAIT_ROWS[0], Z, some_weights)
            experts(0, lambda E: pe_expert_in(pe, E), lambda E: pe_expert_up(pe, E), lambda E: pe_expert_down(pe, E))
            pe.wait_ge(eres_ready, 2 * NE)
            pe.wait_ge(wv_lo, 1)
            pe.wait_ge(wo_lo, 1)
            keep_busy(WAIT_X1, SC[1][1], some_weights)

            last = [None]

            def take(b, kind, u, db):
                if last[0] is not None:
                    k, lu, ldb = last[0]
                    s, per = PJ_READ[k]
                    pe.wait_ge(s, per * (b + ldb) + lu + 1)
                last[0] = (kind, u, db)

            def pe_yT(b, par):
                pe.wait_ge(ya_ready, b + 1)
                for j in range(BT):
                    ins = nc.tensor.transpose(PJ[:, j * P:(j + 1) * P], ya[:, j, :], ident[:])
                ins.then_inc(yT_ps, 1)

            def pe_g(b, p, par):
                if p == 0:
                    pe.wait_ge(yT_lo, b + 1)
                for h in range(2):
                    hh = 2 * p + h
                    o = PJ[:, h * SEQ:(h + 1) * SEQ]
                    nc.tensor.matmul(o, ah[:, hh, :], yTh[par][:], start=True, stop=False)
                    nc.tensor.matmul(o, al[:, hh, :], yTh[par][:], start=False, stop=False)
                    ins = nc.tensor.matmul(o, ah[:, hh, :], yTl[par][:], start=False, stop=True)
                ins.then_inc(g_ps, 1)

            def pe_transpose_probs(b, p, h):
                tb, tp = back(b, p, 2)
                if valid(tb):
                    g = at(tb, tp)
                    if h == 0:
                        pe.wait_ge(prob_ready, g + 1)
                    if not (isinstance(tb, int) and g < 1):
                        pe.wait_ge([pT_even, pT_odd][h], g)
                    for j in range(2):
                        for c in range(2):
                            ins = nc.tensor.transpose(
                                PT[h][:, j * SEQ + c * P:j * SEQ + (c + 1) * P],
                                prob[tp % 4][:, c, h, j * P:(j + 1) * P], ident[:])
                    ins.then_inc(pT_ps, 1)

            def pe_v(b, par, p):
                zb, zp = back(b, p, 4)
                if valid(zb):
                    pe.wait_ge(z_ready, at(zb, zp) + 1)
                elif p:
                    pe.wait_ge(v_ready, p)
                part = slice((p // BT) * SEQ, (p // BT + 1) * SEQ)
                t = slice((p % BT) * P, (p % BT + 1) * P)
                nc.tensor.matmul(VPS, yTh[par][:, t], wvh[:, part], start=True, stop=False)
                nc.tensor.matmul(VPS, yTh[par][:, t], wvl[:, part], start=False, stop=False)
                nc.tensor.matmul(VPS, yTl[par][:, t], wvh[:, part], start=False, stop=True).then_inc(v_ps, 1)

            def pe_o(b, pairs):
                o = o_bank(b)
                for k in pairs:
                    nc.tensor.matmul(o, woh[:, k, :], zh[:, k, :], start=k == 0, stop=False)
                    nc.tensor.matmul(o, wol[:, k, :], zh[:, k, :], start=False, stop=False)
                    ins = nc.tensor.matmul(o, woh[:, k, :], zl[:, k, :], start=False, stop=k == NPAIR - 1)
                return ins

            def middle(b, par, p):
                kind, db = MIDDLE[p]
                tb = b + db
                if not valid(tb):
                    return
                if kind == "yT":
                    take(b, kind, 0, db)
                    pe_yT(tb, 1 - par)
                elif kind == "o":
                    if valid(b):
                        pe.wait_ge(z_lo, at(tb, NPAIR - 1) + 1)
                        take(b, kind, 0, db)
                        pe_o(b, range(NPAIR)).then_inc(o_ps, 1)
                elif kind == "o_back":
                    pe.wait_ge(oT_ready, tb + 1)
                    take(b, kind, 0, db)
                    for c in range(BT):
                        ins = nc.tensor.transpose(PJ[:, c * P:(c + 1) * P], oT[:, c, :], ident[:])
                    ins.then_inc(o_back_ps, 1)
                elif kind == "tT":
                    pe.wait_ge(R[1]["tok_done"], tb + 1)
                    take(b, kind, 0, db)
                    for j in range(BT):
                        ins = nc.tensor.transpose(PJ[:, j * P:(j + 1) * P], rt[1]("row", 0)[:, j, 0:D], ident[:])
                    ins.then_inc(R[1]["tT_ps"], 1)
                elif kind == "logit":
                    pe.wait_ge(R[1]["tT_ready"], tb + 1)
                    take(b, kind, 0, db)
                    for j in range(BT):
                        ins = nc.tensor.matmul(PJ[:, j * NE:(j + 1) * NE], rt[1]("tokT", 0)[:, j, :], gateT[:],
                                               start=True, stop=True)
                    ins.then_inc(R[1]["logit_ps"], 1)
                elif kind == "rank":
                    pe.wait_ge(R[1]["hot_ready"], tb + 1)
                    take(b, kind, 0, db)
                    pe_ranks(1, 0, PJ[:, 0:(BT + 1) * NE].rearrange("p (n e) -> p n e", e=NE)) \
                        .then_inc(R[1]["rank_ps"], 1)

            def batch(b, par):
                for p in range(NPAIR):
                    nb, np_ = fwd(b, p)
                    if valid(nb):
                        take(b, "g", np_, 0 if p + 1 < NPAIR else 1)
                        pe_g(nb, np_, par if p + 1 < NPAIR else 1 - par)
                    if valid(b):
                        g = at(b, p)
                        pe.wait_ge(g_lo, g + 1)
                        if not (isinstance(b, int) and g < 2):
                            pe.wait_ge(exp_done, 2 * g - 2)
                        for c in range(2):
                            if c == 1:
                                pe_v(b, par, p)
                            for h in range(2):
                                o = SC[p % 2][c][:, h * SEQ:(h + 1) * SEQ]
                                q = slice(h * SEQ + c * P, h * SEQ + (c + 1) * P)
                                nc.tensor.matmul(o, Gh[p % 2][:, q], yTh[par][:], start=True, stop=False)
                                nc.tensor.matmul(o, Gh[p % 2][:, q], yTl[par][:], start=False, stop=False)
                                ins = nc.tensor.matmul(o, Gl[p % 2][:, q], yTh[par][:], start=False, stop=True)
                            ins.then_inc(scores_ps, 1)
                    pe_transpose_probs(b, p, 0)
                    if p in MIDDLE:
                        middle(b, par, p)
                    pe_transpose_probs(b, p, 1)
                    zb, zp = back(b, p, 3)
                    if valid(zb):
                        g = at(zb, zp)
                        pe.wait_ge(pT_even, g + 1)
                        pe.wait_ge(pT_odd, g + 1)
                        pe.wait_ge(v_ready, NV * zb + BT * (zp // 2 + 1))
                        if not valid(b) and zp + zb:
                            pe.wait_ge(z_ready, g)
                        if valid(b):
                            pe.wait_ge(v_ready, NV * b + p + 1)
                        for j in range(2):
                            for h in range(2):
                                ins = nc.tensor.matmul(
                                    Z[DK * h:DK * h + DK, 0:SEQ], V[:, j, (2 * zp + h) * DK:(2 * zp + h + 1) * DK],
                                    probT[zp % 2][h][:, j, :], start=j == 0, stop=j == 1)
                        ins.then_inc(z_ps, 1)
                    if valid(b - 1) and not valid(b) and p in O_TAIL:
                        pe.wait_ge(exp_done, 2 * NB * NPAIR)
                        pe.wait_ge(z_lo, at(NB - 1, O_TAIL[p][-1]) + 1)
                        ins = pe_o(b, O_TAIL[p])
                        if p == 3:
                            ins.then_inc(o_ps, 1)
                    if not valid(b) and valid(b - 1) and p == 4:
                        keep_busy(WAIT_NORM, SC[1][1], some_weights)
                k, u, db = last[0]
                last[0] = (k, u, db - 1)
            take(0, "yT", 0, 0)
            pe_yT(0, 0)
            take(0, "g", 0, 0)
            pe_g(0, 0, 0)
            run(pe, batch)
            pe.wait_ge(R[1]["rank_read"], NB)
            keep_busy(WAIT_ROWS[1], Z, some_weights)
            experts(1, lambda E: pe_expert_in(pe, E), lambda E: pe_expert_up(pe, E), lambda E: pe_expert_down(pe, E))


_INS = ["x", "w_qT", "w_kT", "w_v", "w_o", "gate", "gamma", "beta", "wi", "wo", "ident", "before", "ebase", "rev",
        "noslot", "tokid", "empty"]


def kernel(**inputs):
    from concourse import bacc as _bacc
    from concourse.bass_utils import run_bass_kernel_spmd as _run

    a = {k: np.asarray(v) for k, v in inputs.items()}
    p = np.arange(P)
    data = {
        "x": a["L0_attn_x"],
        "w_qT": a["L0_attn_w_q"].transpose(0, 2, 1).reshape(NH * DK, D),
        "w_kT": a["L0_attn_w_k"].transpose(0, 2, 1).reshape(NH * DK, D),
        "w_v": a["L0_attn_w_v"].transpose(1, 0, 2).reshape(D, NH * DK),
        "w_o": a["L0_attn_w_o"],
        "gate": a["L0_ffn_gate_weight"].T,
        "gamma": a["L0_ffn_ln_gamma"].reshape(D, 1),
        "beta": a["L0_ffn_ln_beta"].reshape(D, 1),
        "wi": a["L0_ffn_wi"],
        "wo": a["L0_ffn_wo"],
        "ident": np.eye(P, dtype=np.float32),
        "before": np.triu(np.ones((P, P), np.float32), 1),
        "ebase": np.tile(np.arange(NE, dtype=np.float32) * CAP, (P, 1)),
        "rev": np.tile(np.arange(NE, 0, -1, dtype=np.float32), (P, 1)),
        "noslot": (NOSLOT + np.arange(GT)[None, :] * P + p[:, None]).astype(np.float32),
    }
    data["tokid"] = (np.arange(NT)[None, :] * P + p[:, None]).astype(np.float32)
    data["empty"] = np.zeros((P, 4, ROW), np.float32)
    data["empty"][:, :, ROW_ID] = NOTOK + p[:, None]
    nc = _bacc.Bacc("TRN2", target_bir_lowering=False, num_devices=1)
    arrays, args = {}, []
    for name in _INS:
        v = np.ascontiguousarray(data[name])
        arrays[f"in_{name}_dram"] = v
        args.append(nc.dram_tensor(f"in_{name}_dram", v.shape, mybir.dt.from_np(v.dtype), kind="ExternalInput").ap())
    out = nc.dram_tensor("out_0_dram", (NB, SEQ, D), F32, kind="ExternalOutput").ap()
    macaron_kernel(nc, *args, out)
    r = _run(nc, [arrays], core_ids=[0])
    return r.results[0]["out_0_dram"]
```
